# Optimizing a Trainium2 kernel written in Bass

```python
import numpy as np
import jax
import jax.numpy as jnp

def _softmax(x, axis=-1):
    return jax.nn.softmax(x, axis=axis)

def _gelu(x):
    return jax.nn.gelu(x, approximate=True)

def _silu(x):
    return jax.nn.silu(x)

def _sigmoid(x):
    return jax.nn.sigmoid(x)

def _layernorm(x, axis=-1, eps=1e-05):
    m = jnp.mean(x, axis=axis, keepdims=True)
    v = jnp.var(x, axis=axis, keepdims=True)
    return (x - m) / jnp.sqrt(v + eps)

def _scatter_add(tgt, idx, src, axis=0):
    return tgt.at[idx].add(src)

def _segment_sum(src, seg, n):
    return jax.ops.segment_sum(src, seg, n)
kernel_name = 'mk_vit_tower_d1_tok_img768_r4_bb1511'

def setup_inputs(seed: int=0):
    np.random.seed(seed)
    _w = jnp.asarray

    def _rec_inputs():
        import jax
        import jax.numpy as jnp
        _rk = jax.random.key(seed)
        x = -0.00016672 + 0.999947 * jax.random.normal(jax.random.fold_in(_rk, 1), (16, 3, 96, 96), jnp.float32)
        return x
    x = _rec_inputs()

    def _L0_tok_setup():
        import jax, jax.numpy as jnp
        import numpy as np
        EPS = 1e-05
        PH = PW = 16

        def _layernorm(x, w, b):
            mu = jnp.mean(x, axis=-1, keepdims=True)
            var = jnp.mean(jnp.square(x - mu), axis=-1, keepdims=True)
            return (x - mu) * jax.lax.rsqrt(var + EPS) * w + b
        key = jax.random.key(seed)
        ks = jax.random.split(key, 4)
        B, C, H, Wimg = (64, 3, 96, 96)
        D = 192
        pd = PH * PW * C
        seq = H // PH * (Wimg // PW)
        return {'x': jax.random.normal(ks[0], (B, C, H, Wimg), dtype=jnp.float32), 'ln1_w': jnp.ones((pd,), jnp.float32), 'ln1_b': jnp.zeros((pd,), jnp.float32), 'W': jax.random.normal(ks[1], (pd, D), dtype=jnp.float32) * (1.0 / np.sqrt(pd)), 'b': jnp.zeros((D,), jnp.float32), 'ln2_w': jnp.ones((D,), jnp.float32), 'ln2_b': jnp.zeros((D,), jnp.float32), 'cls': jax.random.normal(ks[2], (1, D), dtype=jnp.float32), 'pos': jnp.zeros((seq + 1, D), jnp.float32)}
    _L0_tok_all = _L0_tok_setup()
    _L0_tok_in = {k: v for k, v in _L0_tok_all.items() if k in ('ln1_w', 'ln1_b', 'W', 'b', 'ln2_w', 'ln2_b', 'cls', 'pos')}
    del _L0_tok_all

    def _L0_attn_setup():
        import jax, jax.numpy as jnp
        import numpy as np
        DIM = 192
        D_STATE = 16
        D_CONV = 4
        EXPAND = 2
        E = DIM * EXPAND
        EPS = 1e-06
        key = jax.random.key(seed)
        ks = jax.random.split(key, 9)
        B, L = (2, 512)
        s = lambda *sh: 0.02
        return {'x': jax.random.normal(ks[0], (B, L, DIM), jnp.float32), 'gamma': jnp.ones((DIM,), jnp.float32), 'W_in': jax.random.normal(ks[1], (E, DIM), jnp.float32) * 0.02, 'b_in': jax.random.normal(ks[2], (E,), jnp.float32) * 0.02, 'conv_w': jax.random.normal(ks[3], (E, D_CONV), jnp.float32) * 0.1, 'A': jax.random.normal(ks[4], (E, D_STATE), jnp.float32) * 0.1, 'Bp': jax.random.normal(ks[5], (E, D_STATE), jnp.float32) * 0.1, 'C': jax.random.normal(ks[6], (E, D_STATE), jnp.float32) * 0.1, 'W_out': jax.random.normal(ks[7], (DIM, E), jnp.float32) * 0.02, 'b_out': jax.random.normal(ks[8], (DIM,), jnp.float32) * 0.02}
    _L0_attn_all = _L0_attn_setup()
    _L0_attn_in = {k: v for k, v in _L0_attn_all.items() if k in ('gamma', 'W_in', 'b_in', 'conv_w', 'A', 'Bp', 'C', 'W_out', 'b_out')}
    del _L0_attn_all

    def _L0_ffn_setup():
        import jax, jax.numpy as jnp
        import numpy as np
        GT0 = [[0, 1, 0, 0, 1, 0], [0, 1, 0, 0, 0, 1], [0, 0, 1, 0, 1, 0], [0, 0, 1, 0, 0, 1], [0, 0, 0, 1, 1, 0], [0, 0, 0, 1, 0, 1]]
        NCLS = 6
        K = 1

        def _expert_pairs():
            pairs = []
            for i in range(NCLS):
                p = [(j - 1, k - 1) for j in range(1, 6) for k in range(1, 6) if j != k and GT0[i][j] == 1 and (GT0[i][k] == 1)]
                pairs.append(p)
            return pairs
        PAIRS = _expert_pairs()
        B, P, D, H = (64, 64, 192, 768)

        def _gelu(t):
            return jax.nn.gelu(t, approximate=False)
        key = jax.random.key(seed)
        ks = jax.random.split(key, 8)
        s = 0.02
        x = jax.random.normal(ks[0], (B, NCLS + P, D), dtype=jnp.float32)
        mids = jax.random.randint(ks[1], (B,), 0, 6)
        moe0_W1 = jax.random.normal(ks[2], (D, H), dtype=jnp.float32) * s
        moe0_b1 = jnp.zeros((H,), jnp.float32)
        moe0_W2 = jax.random.normal(ks[3], (H, D), dtype=jnp.float32) * s
        moe0_b2 = jnp.zeros((D,), jnp.float32)
        A1_W = jax.random.normal(ks[4], (5, D, H), dtype=jnp.float32) * s
        A1_b = jnp.zeros((5, H), jnp.float32)
        A2_W = jax.random.normal(ks[5], (5, H, D), dtype=jnp.float32) * s
        A2_b = jnp.zeros((5, D), jnp.float32)
        G_W = jax.random.normal(ks[6], (NCLS, D, 2), dtype=jnp.float32) * s
        return {'x': x, 'moe0_W1': moe0_W1, 'moe0_b1': moe0_b1, 'moe0_W2': moe0_W2, 'moe0_b2': moe0_b2, 'A1_W': A1_W, 'A1_b': A1_b, 'A2_W': A2_W, 'A2_b': A2_b, 'G_W': G_W, 'mids': mids}
    _L0_ffn_all = _L0_ffn_setup()
    _L0_ffn_in = {k: v for k, v in _L0_ffn_all.items() if k in ('moe0_W1', 'moe0_b1', 'moe0_W2', 'moe0_b2', 'A1_W', 'A1_b', 'A2_W', 'A2_b', 'G_W', 'mids')}
    del _L0_ffn_all
    return {'x': x, 'L0_tok_ln1_w': _L0_tok_in['ln1_w'], 'L0_tok_ln1_b': _L0_tok_in['ln1_b'], 'L0_tok_W': _L0_tok_in['W'], 'L0_tok_b': _L0_tok_in['b'], 'L0_tok_ln2_w': _L0_tok_in['ln2_w'], 'L0_tok_ln2_b': _L0_tok_in['ln2_b'], 'L0_tok_cls': _L0_tok_in['cls'], 'L0_tok_pos': _L0_tok_in['pos'], 'L0_attn_gamma': _L0_attn_in['gamma'], 'L0_attn_W_in': _L0_attn_in['W_in'], 'L0_attn_b_in': _L0_attn_in['b_in'], 'L0_attn_conv_w': _L0_attn_in['conv_w'], 'L0_attn_A': _L0_attn_in['A'], 'L0_attn_Bp': _L0_attn_in['Bp'], 'L0_attn_C': _L0_attn_in['C'], 'L0_attn_W_out': _L0_attn_in['W_out'], 'L0_attn_b_out': _L0_attn_in['b_out'], 'L0_ffn_moe0_W1': _L0_ffn_in['moe0_W1'], 'L0_ffn_moe0_b1': _L0_ffn_in['moe0_b1'], 'L0_ffn_moe0_W2': _L0_ffn_in['moe0_W2'], 'L0_ffn_moe0_b2': _L0_ffn_in['moe0_b2'], 'L0_ffn_A1_W': _L0_ffn_in['A1_W'], 'L0_ffn_A1_b': _L0_ffn_in['A1_b'], 'L0_ffn_A2_W': _L0_ffn_in['A2_W'], 'L0_ffn_A2_b': _L0_ffn_in['A2_b'], 'L0_ffn_G_W': _L0_ffn_in['G_W'], 'L0_ffn_mids': _L0_ffn_in['mids']}

def reference(x, L0_tok_ln1_w, L0_tok_ln1_b, L0_tok_W, L0_tok_b, L0_tok_ln2_w, L0_tok_ln2_b, L0_tok_cls, L0_tok_pos, L0_attn_gamma, L0_attn_W_in, L0_attn_b_in, L0_attn_conv_w, L0_attn_A, L0_attn_Bp, L0_attn_C, L0_attn_W_out, L0_attn_b_out, L0_ffn_moe0_W1, L0_ffn_moe0_b1, L0_ffn_moe0_W2, L0_ffn_moe0_b2, L0_ffn_A1_W, L0_ffn_A1_b, L0_ffn_A2_W, L0_ffn_A2_b, L0_ffn_G_W, L0_ffn_mids):
    import jax
    import jax.numpy as jnp

    def _L0_tok_ref(x, ln1_w, ln1_b, W, b, ln2_w, ln2_b, cls, pos):
        import jax, jax.numpy as jnp
        import numpy as np
        EPS = 1e-05
        PH = PW = 16

        def _layernorm(x, w, b):
            mu = jnp.mean(x, axis=-1, keepdims=True)
            var = jnp.mean(jnp.square(x - mu), axis=-1, keepdims=True)
            return (x - mu) * jax.lax.rsqrt(var + EPS) * w + b
        B, C, H, Wimg = x.shape
        nh, nw = (H // PH, Wimg // PW)
        p = x.reshape(B, C, nh, PH, nw, PW)
        p = jnp.transpose(p, (0, 2, 4, 3, 5, 1)).reshape(B, nh * nw, PH * PW * C)
        h = _layernorm(p, ln1_w, ln1_b)
        h = jnp.einsum('bsp,pd->bsd', h, W) + b
        h = _layernorm(h, ln2_w, ln2_b)
        cls_tok = jnp.broadcast_to(cls[None, :, :], (B, 1, cls.shape[-1]))
        out = jnp.concatenate([cls_tok, h], axis=1) + pos
        return out

    def _L0_attn_ref(x, gamma, W_in, b_in, conv_w, A, Bp, C, W_out, b_out):
        import jax, jax.numpy as jnp
        import numpy as np
        DIM = 192
        D_STATE = 16
        D_CONV = 4
        EXPAND = 2
        E = DIM * EXPAND
        EPS = 1e-06
        residual = x
        rms = jnp.linalg.norm(x, axis=-1, keepdims=True) * x.shape[-1] ** (-0.5)
        xn = gamma * (x / (rms + EPS))
        xp = xn @ W_in.T + b_in
        B_, L_, _ = xp.shape
        pad = D_CONV - 1
        xpad = jnp.pad(xp, ((0, 0), (pad, 0), (0, 0)))
        xc = jnp.zeros_like(xp)
        for k in range(D_CONV):
            xc = xc + xpad[:, k:k + L_, :] * conv_w[:, k]
        sigA = jax.nn.sigmoid(A)
        sigB = jax.nn.sigmoid(Bp)
        sigC = jax.nn.sigmoid(C)

        def step(h, xt):
            h = sigA * h + sigB * xt[:, :, None]
            y = jnp.einsum('ben,en->be', h, sigC)
            return (h, y)
        h0 = jnp.zeros((B_, E, D_STATE), xp.dtype)
        _, ys = jax.lax.scan(step, h0, jnp.swapaxes(xc, 0, 1))
        y = jnp.swapaxes(ys, 0, 1)
        out = y @ W_out.T + b_out
        return out + residual

    def _L0_ffn_ref(x, moe0_W1, moe0_b1, moe0_W2, moe0_b2, A1_W, A1_b, A2_W, A2_b, G_W, mids):
        import jax, jax.numpy as jnp
        import numpy as np
        GT0 = [[0, 1, 0, 0, 1, 0], [0, 1, 0, 0, 0, 1], [0, 0, 1, 0, 1, 0], [0, 0, 1, 0, 0, 1], [0, 0, 0, 1, 1, 0], [0, 0, 0, 1, 0, 1]]
        NCLS = 6
        K = 1

        def _expert_pairs():
            pairs = []
            for i in range(NCLS):
                p = [(j - 1, k - 1) for j in range(1, 6) for k in range(1, 6) if j != k and GT0[i][j] == 1 and (GT0[i][k] == 1)]
                pairs.append(p)
            return pairs
        PAIRS = _expert_pairs()
        B, P, D, H = (64, 64, 192, 768)

        def _gelu(t):
            return jax.nn.gelu(t, approximate=False)
        cls_tokens = x[:, :NCLS]
        patch_tokens = x[:, NCLS:]
        patch_out = _gelu(patch_tokens @ moe0_W1 + moe0_b1) @ moe0_W2 + moe0_b2
        cls_outs = []
        for i in range(NCLS):
            tok = cls_tokens[:, i]
            eouts = [_gelu(tok @ A1_W[a] + A1_b[a]) @ A2_W[c] + A2_b[c] for a, c in PAIRS[i]]
            out = jnp.stack(eouts, axis=-1)
            gate = jax.nn.softmax(tok @ G_W[i], axis=-1)
            thr = jnp.sort(gate, axis=-1)[..., -(K + 1)]
            mask = (gate > thr[..., None]).astype(gate.dtype)
            g = gate * mask
            g = g / jnp.clip(jnp.sum(g, axis=-1, keepdims=True), 1e-06)
            cls_outs.append(jnp.sum(out * g[:, None, :], axis=-1))
        cls_out = jnp.stack(cls_outs, axis=1)
        return jnp.concatenate([cls_out, patch_out], axis=1)
    h = _L0_tok_ref(x, L0_tok_ln1_w, L0_tok_ln1_b, L0_tok_W, L0_tok_b, L0_tok_ln2_w, L0_tok_ln2_b, L0_tok_cls, L0_tok_pos)
    h = h + _L0_attn_ref(_layernorm(h, axis=-1), L0_attn_gamma, L0_attn_W_in, L0_attn_b_in, L0_attn_conv_w, L0_attn_A, L0_attn_Bp, L0_attn_C, L0_attn_W_out, L0_attn_b_out)
    h = h + _L0_ffn_ref(_layernorm(h, axis=-1), L0_ffn_moe0_W1, L0_ffn_moe0_b1, L0_ffn_moe0_W2, L0_ffn_moe0_b2, L0_ffn_A1_W, L0_ffn_A1_b, L0_ffn_A2_W, L0_ffn_A2_b, L0_ffn_G_W, L0_ffn_mids)
    return h

_drawn_inputs = setup_inputs


def setup_inputs(seed=0):
    import zlib

    import numpy as np

    out = dict(_drawn_inputs(seed))
    spreads = {'L0_tok_ln1_w': (1.0, 0.2),
     'L0_tok_ln1_b': (0.0, 0.1),
     'L0_tok_b': (0.0, 0.1),
     'L0_tok_ln2_w': (1.0, 0.2),
     'L0_tok_ln2_b': (0.0, 0.1),
     'L0_tok_pos': (0.0, 0.1),
     'L0_attn_gamma': (1.0, 0.6),
     'L0_ffn_moe0_b1': (0.0, 0.607),
     'L0_ffn_moe0_b2': (0.0, 0.1),
     'L0_ffn_A1_b': (0.0, 0.8),
     'L0_ffn_A2_b': (0.0, 0.402)}
    factors = {'L0_attn_b_in': 8.0,
     'L0_attn_A': 49.505,
     'L0_attn_Bp': 48.932,
     'L0_attn_C': 53.753,
     'L0_attn_b_out': 5.365,
     'L0_ffn_A1_W': 3.613,
     'L0_ffn_A2_W': 3.29,
     'L0_ffn_G_W': 3.632}
    for name, (base, spread) in spreads.items():
        noise = np.random.default_rng([zlib.crc32(name.encode()), seed]).standard_normal(out[name].shape)
        drawn = base * np.exp(spread * noise) if base else spread * noise
        out[name] = jnp.asarray(drawn.astype(out[name].dtype))
    for name, factor in factors.items():
        out[name] = (out[name] * factor).astype(out[name].dtype)
    return out
```

```python
import concourse.bass as bass
from concourse import mybir
from contextlib import ExitStack


def vit_tower_kernel(nc, x, ln1_w, ln1_b, tok_W, tok_b, ln2_w, ln2_b, cls, pos,
                     gamma, W_in, b_in, conv_w, A, Bp, C, W_out, b_out,
                     m0_W1, m0_b1, m0_W2, m0_b2, A1_W, A1_b, A2_W, A2_b, G_W, out):
    F32 = mybir.dt.float32
    ALU = mybir.AluOpType
    ACT = mybir.ActivationFunctionType
    AX = mybir.AxisListType
    MUL, ADD, SUB = ALU.mult, ALU.add, ALU.subtract

    NB, NC, IMG, _ = x.shape
    P = 16
    NH = NW = IMG // P
    BH = NB * NH
    D = tok_W.shape[1]
    DH = D // 2
    T = NH * NW + 1
    NT = NB * T
    E = W_in.shape[0]
    ET = E // 128
    NST = A.shape[1]
    DC = conv_w.shape[1]
    NCLS = 6
    CT = NCLS * NB
    PT = NT - CT
    HID = m0_W1.shape[1]
    M = HID // 128
    NEXP = A1_W.shape[0]
    HB = 8
    H2 = P // HB
    KC = NC * H2
    EPS5, EPS6 = 1e-5, 1e-6
    SPLIT = 19 * NB
    PTILES = [(0, 128), (128, 128), (256, 128), (384, PT - 384)]
    HALF = [(0, 256), (256, PT - 256)]
    LO = [0, 0, 1, 1, 2, 2]
    HI = [3, 4, 3, 4, 3, 4]
    PE_TAPS = [0, 3, 6, 9, 12, 15, 18, 21, 24, 27, 30, 33, 36]
    PE_PARTS = [5, 3, 3, 2]
    VE_TAPS = [k for k in range(T) if k not in PE_TAPS]
    VE_PARTS = [5, 3, 2, 8, 6]
    assert PE_TAPS[0] * NB <= CT and VE_TAPS[0] * NB <= CT
    NDG = len(PE_TAPS)

    ctx = ExitStack()
    with ctx:
        def sb(name, shape):
            return ctx.enter_context(nc.sbuf_tensor(name, shape, F32))

        def within(area, offset, shape):
            n = 1
            for d in shape[1:]:
                n *= d
            v = area[0:shape[0], offset:offset + n]
            if len(shape) > 2:
                names = "abcd"[:len(shape) - 1]
                v = v.rearrange(f"p ({' '.join(names)}) -> p {' '.join(names)}",
                                **{k: d for k, d in zip(names[1:], shape[2:])})
            return v

        def sem(name):
            return ctx.enter_context(nc.semaphore(name))

        ident = sb("ident", [128, 128])
        ones = sb("ones", [1, 128])
        sel01 = sb("sel01", [1, 2])
        sel_rows = sb("sel_rows", [2, 2, 128])
        half_exp = sb("half_exp", [128, 2, 8])
        pixel_area = sb("pixel_area", [128, NC * P * IMG])
        x_sb = within(pixel_area, 0, [BH, NC, P * IMG])
        hid = within(pixel_area, 0, [128, M, PT])
        hidc = within(pixel_area, M * PT, [128, 2, M, CT])
        W_sb = sb("W_sb", [128, H2, NC, D])
        Wp_area = sb("Wp_area", [128, KC * D])
        Wp = within(Wp_area, 0, [128, H2, NC, D])
        o = within(Wp_area, 0, [128, 4, D])
        ln1_rows = sb("ln1_rows", [4, 128 * NC])
        ln1_col = sb("ln1_col", [128, NC, 4])
        tokb_row = sb("tokb_row", [1, D])
        fold_rows = sb("fold_rows", [2, D])
        fold_bc = sb("fold_bc", [BH, 2, D])
        bias_rows = sb("bias_rows", [NEXP * M + M + ET, 128])
        bias_col = sb("bias_col", [128, NEXP * M + M + ET])
        half_rows = sb("half_rows", [2 * NEXP + 2, DH])
        half_col = sb("half_col", [DH, 2 * NEXP + 2])
        ssm = sb("ssm", [128, 3, ET, NST])
        cw = sb("cw", [128, ET, DC])
        seq_area = sb("seq_area", [128, ET * NT])
        powr = within(seq_area, 0, [128, T, ET * NST])
        xp = within(seq_area, 0, [128, ET, NT])
        sq = sb("sq", [128, 6, ET * NST])
        Gk = sb("Gk", [128, T, ET])
        Kk = sb("Kk", [128, T, ET])
        ktmp = sb("ktmp", [128, DC, T, ET])
        diag = sb("diag", [128, NDG, ET, 128])
        line_area = sb("line_area", [128, NEXP * M * D])
        xr = within(line_area, 0, [BH, KC, NW, 128])
        A2_sb = within(line_area, 0, [128, NEXP, M, D])
        xT_area = sb("xT_area", [128, KC * NW * BH])
        xT = within(xT_area, 0, [128, KC, NW, BH])
        h3 = within(xT_area, 0, [128, 5, D])
        h3b = within(xT_area, 5 * D, [128, 5, D])
        x4 = within(xT_area, 10 * D, [128, 5, D])
        ln2w_bc = sb("ln2w_bc", [BH, D])
        ln2b_bc = sb("ln2b_bc", [BH, D])
        posb = sb("posb", [BH, NW, D])
        bout_bc = sb("bout_bc", [128, D])
        m0b2_bc = sb("m0b2_bc", [128, D])
        cls_sb = sb("cls_sb", [NB, D])
        pos0_sb = sb("pos0_sb", [NB, D])
        st1 = sb("st1", [BH, NW, NC, 6])
        ag1 = sb("ag1", [BH, NW, 2])
        ve1 = sb("ve1", [BH, NW])
        rs1 = sb("rs1", [BH, NW])
        nm1 = sb("nm1", [BH, NW])
        tok_area = sb("tok_area", [128, 2 * NW * D])
        ub = within(tok_area, 0, [BH, NW, D])
        h = within(tok_area, NW * D, [BH, NW, D])
        y = within(tok_area, 0, [128, ET, NT])
        st2 = sb("st2", [BH, NW, 6])
        ag2 = sb("ag2", [BH, NW, 2])
        ve2 = sb("ve2", [BH, NW])
        rs2 = sb("rs2", [BH, NW])
        h2 = sb("h2", [BH, NW + 1, D])
        st3 = sb("st3", [BH, NW + 1, 6])
        ag3 = sb("ag3", [BH, NW + 1, 2])
        ve3 = sb("ve3", [BH, 2, NW + 1])
        rs3 = sb("rs3", [BH, 2, NW + 1])
        rms3 = sb("rms3", [BH, NW + 1])
        sc3 = sb("sc3", [BH, NW + 1])
        one3 = sb("one3", [BH, NW + 1])
        nm3 = sb("nm3", [BH, NW + 1])
        xs = sb("xs", [BH, NW + 1, D])
        r = sb("r", [BH, NW + 1, D])
        Win_sb = sb("Win_sb", [128, ET, D])
        Wout_sb = sb("Wout_sb", [DH, 2, E])
        WinT = sb("WinT", [DH, 2, E])
        WoutT = sb("WoutT", [128, ET, D])
        xnT = sb("xnT", [DH, 2, NT])
        r_tok = sb("r_tok", [128, 5, D])
        st4 = sb("st4", [128, 5, 6])
        ag4 = sb("ag4", [128, 5, 2])
        ve4 = sb("ve4", [128, 5])
        rs4 = sb("rs4", [128, 5])
        x4T = sb("x4T", [DH, 2, NT])
        A1_sb = sb("A1_sb", [DH, NEXP, 2, HID])
        W1_sb = sb("W1_sb", [DH, 2, HID])
        W2_sb = sb("W2_sb", [128, M, D])
        G_sb = sb("G_sb", [DH, 2, NCLS, 2])
        cmask = sb("cmask", [CT, NCLS])
        gsel = sb("gsel", [CT, NCLS, 2])
        lg = sb("lg", [CT, 2])
        g_mx = sb("g_mx", [CT, 1])
        g_d = sb("g_d", [CT, 2])
        g_e = sb("g_e", [CT, 2])
        g_s = sb("g_s", [CT, 1])
        g_p = sb("g_p", [CT, 2])
        g_m = sb("g_m", [CT, 2])
        gate = sb("gate", [CT, 2])
        oTc = sb("oTc", [DH, 2, 2, CT])
        oc1 = sb("oc1", [CT, D])
        oc = sb("oc", [CT, D])
        ps = ctx.enter_context(nc.psum_tensor("ps", [128, 8, 512], F32))
        r_dram = nc.dram_tensor("r_scratch", [NT, D], F32).ap()

        l_ln1 = sem("l_ln1")
        l_ssm = sem("l_ssm")
        l_W = sem("l_W")
        l_x = [sem(f"l_x{c}") for c in range(NC)]
        l_tokb = sem("l_tokb")
        l_rows = sem("l_rows")
        l_half = sem("l_half")
        l_cls = sem("l_cls")
        l_ln2 = sem("l_ln2")
        l_pos = sem("l_pos")
        l_bc = sem("l_bc")
        l_Win = sem("l_Win")
        l_Wout = sem("l_Wout")
        l_G = sem("l_G")
        l_A1 = sem("l_A1")
        l_A2 = sem("l_A2")
        l_W1 = sem("l_W1")
        l_W2 = sem("l_W2")
        s_rw = sem("s_rw")
        l_rc = sem("l_rc")
        l_rp = sem("l_rp")
        s_out = sem("s_out")
        pool_step = sem("pool_step")
        ident_ready = sem("ident_ready")
        const_ready = sem("const_ready")
        posb_ready = sem("posb_ready")
        pow0 = sem("pow0")
        pow1 = sem("pow1")
        pow2 = sem("pow2")
        pow3 = sem("pow3")
        pow4 = sem("pow4")
        diag_ready = sem("diag_ready")
        rtok_ready = sem("rtok_ready")
        h3b_ready = sem("h3b_ready")
        vec_step = sem("vec_step")
        Wp_ready = sem("Wp_ready")
        K_ready = sem("K_ready")
        var0 = sem("var0")
        var1 = sem("var1")
        var2 = sem("var2")
        var3 = sem("var3")
        var4 = sem("var4")
        ln1c_ready = sem("ln1c_ready")
        h_read = sem("h_read")
        rc_ready = sem("rc_ready")
        xs_ready = sem("xs_ready")
        ycls_ready = sem("ycls_ready")
        y_ready = sem("y_ready")
        h3_ready = sem("h3_ready")
        x4_ready = sem("x4_ready")
        gmax_ready = sem("gmax_ready")
        oc_ready = sem("oc_ready")
        o_ready = sem("o_ready")
        sig_ready = sem("sig_ready")
        rows_ready = sem("rows_ready")
        fold_ready = sem("fold_ready")
        cols_ready = sem("cols_ready")
        xr_ready = sem("xr_ready")
        xT_ready = sem("xT_ready")
        wT_ready = sem("wT_ready")
        r_ready = sem("r_ready")
        xnT_ready = sem("xnT_ready")
        xp_ready = sem("xp_ready")
        x4T_ready = sem("x4T_ready")
        gexp_ready = sem("gexp_ready")
        hidc_ready = sem("hidc_ready")
        oTc_ready = sem("oTc_ready")
        hid_ready = sem("hid_ready")
        t_ln1 = sem("t_ln1")
        t_rows = sem("t_rows")
        t_fold = sem("t_fold")
        t_cols = sem("t_cols")
        t_x = sem("t_x")
        t_h = sem("t_h")
        t_w = sem("t_w")
        t_xs = sem("t_xs")
        t_xp = sem("t_xp")
        t_y = sem("t_y")
        t_woc = sem("t_woc")
        t_wo = sem("t_wo")
        t_x4c = sem("t_x4c")
        t_x4 = sem("t_x4")
        t_g = sem("t_g")
        t_upc = sem("t_upc")
        t_dnc = sem("t_dnc")
        t_oc = sem("t_oc")
        t_up = sem("t_up")
        t_dn = sem("t_dn")

        W_IN_COL = NEXP * M + M
        M0_COL = NEXP * M
        GAMMA_COL = 2 * NEXP
        chunks = [(c, hh) for c in range(NC) for hh in range(H2)]
        x_pix = x_sb[:, :, :].rearrange("p c (y n w) -> p c y n w", y=P, n=NW)
        WO_BANK = [6, 1, 5, 7]
        X4_BANK = [2, 3, 4, 0]
        UP_BANK = [2, 3, 4, 0]
        Y_BANK = [2, 3, 4]
        XP_BANK = [4, 5, 6, 7, 0, 1]

        def hbank(nw):
            return ps[0:BH, 4 + nw // 2, (nw % 2) * D:(nw % 2 + 1) * D]

        def col(v, k):
            return v[:, k:k + 1]

        block = ctx.enter_context(nc.Block())

        @block.sync
        def _(sp):
            sp.dma_start(ln1_rows[0:2, :], ln1_w.rearrange("(h f) -> h f", h=H2)).then_inc(l_ln1, 16)
            sp.dma_start(ln1_rows[2:4, :], ln1_b.rearrange("(h f) -> h f", h=H2)).then_inc(l_ln1, 16)
            sp.dma_start(W_sb[:, :, :, :].rearrange("p h c d -> p h (c d)"),
                         tok_W.rearrange("(h p c) d -> p h (c d)", h=H2, c=NC)).then_inc(l_W, 16)
            for c in range(NC):
                sp.dma_start(x_sb[:, c, :], x[:, c].rearrange("b (n q) w -> b n (q w)", n=NH)).then_inc(l_x[c], 16)
            sp.dma_start(Win_sb[:, :, :], W_in.rearrange("(e p) d -> p e d", p=128)).then_inc(l_Win, 16)
            sp.dma_start(Wout_sb[:, :, :], W_out.rearrange("(h p) e -> p h e", p=DH)).then_inc(l_Wout, 16)
            for hh in range(2):
                sp.dma_start(G_sb[:, hh], G_W[:, hh * DH:(hh + 1) * DH, :].rearrange("i p j -> p i j")
                             ).then_inc(l_G, 16)
            for a in range(NEXP):
                sp.dma_start(A1_sb[:, a], A1_W[a].rearrange("(h p) f -> p h f", p=DH)).then_inc(l_A1, 16)
            sp.wait_ge(t_x, KC)
            for a in range(NEXP):
                sp.dma_start(A2_sb[:, a], A2_W[a].rearrange("(m p) d -> p m d", p=128)).then_inc(l_A2, 16)
            sp.dma_start(W1_sb[:, :, :], m0_W1.rearrange("(h p) f -> p h f", p=DH)).then_inc(l_W1, 16)
            sp.dma_start(W2_sb[:, :, :], m0_W2.rearrange("(m p) d -> p m d", p=128)).then_inc(l_W2, 16)
            r_rows = r_dram.rearrange("(t b) d -> t b d", b=NB)
            sp.wait_ge(r_ready, 1)
            sp.dma_start(r_rows[0], r[0:NB, NW, :]).then_inc(s_rw, 16)
            for nw in range(NW):
                sp.wait_ge(r_ready, nw + 2)
                sp.dma_start(r_rows[1 + nw:T:NW].rearrange("n b d -> b n d"), r[:, nw, :]).then_inc(s_rw, 16)
            sp.wait_ge(s_rw, 16 * (NW + 1))
            sp.dma_start(r_tok[0:CT, 4, :], r_dram[0:CT]).then_inc(l_rc, 16)
            sp.dma_start(r_tok[:, 0:3, :], r_dram[CT:CT + 384].rearrange("(j p) d -> p j d", p=128)
                         ).then_inc(l_rp, 16)
            sp.dma_start(r_tok[0:PTILES[3][1], 3, :], r_dram[CT + 384:NT]).then_inc(l_rp, 16)
            o_rows = out.rearrange("b t d -> t b d")
            sp.wait_ge(oc_ready, 1)
            sp.dma_start(o_rows[0:NCLS], oc[:, :]).then_inc(s_out, 16)
            for j, (c0, n) in enumerate(PTILES):
                t0 = NCLS + c0 // NB
                sp.wait_ge(o_ready, j + 1)
                sp.dma_start(o_rows[t0:t0 + n // NB], o[0:n, j, :]).then_inc(s_out, 16)
            sp.wait_ge(s_out, 16 * 5)

        @block.gpsimd
        def _(pool):
            g = nc.gpsimd
            g.memset(ident[:, :], 0.0).then_inc(pool_step, 1)
            pool.wait_ge(pool_step, 1)
            g.affine_select(out=ident[:, :], in_=ident[:, :], compare_op=ALU.not_equal, fill=1.0,
                            base=0, pattern=[[-1, 128]], channel_multiplier=1).then_inc(ident_ready, 1)
            g.memset(ones[:, :], 1.0).then_inc(const_ready, 1)
            g.memset(sel01[:, 0:1], 0.0).then_inc(const_ready, 1)
            g.memset(sel01[:, 1:2], 1.0).then_inc(const_ready, 1)
            g.memset(half_exp[:, 0, :], -0.5).then_inc(const_ready, 1)
            g.memset(half_exp[:, 1, :], 0.5).then_inc(const_ready, 1)
            pool.wait_ge(ident_ready, 1)
            g.tensor_scalar(sel_rows[:, :, :], ident[0:2, 0:2].unsqueeze(2).broadcast_to([2, 2, 128]),
                            1.0, 1.0, MUL, MUL).then_inc(const_ready, 1)
            pool.wait_ge(const_ready, 6)
            pool.wait_ge(var0, 1)
            g.tensor_tensor(rs3[0:NB, :, NW], ve3[0:NB, :, NW], half_exp[0:NB, :, 0], ALU.pow).then_inc(pow0, 1)
            pool.wait_ge(l_pos, 16)
            pool.wait_ge(l_ln2, 32)
            g.tensor_tensor(posb[:, :, :], posb[:, :, :], ln2b_bc[:, :].unsqueeze(1).broadcast_to([BH, NW, D]),
                            ADD).then_inc(posb_ready, 1)
            pool.wait_ge(K_ready, 1)
            for i, k in enumerate(PE_TAPS):
                for e in range(ET):
                    if i == len(PE_TAPS) // 2 and e == 0:
                        pool.wait_ge(var1, 1)
                        g.tensor_tensor(rs1[:, :], ve1[:, :], half_exp[0:BH, 0, 0:NW], ALU.pow).then_inc(pow1, 1)
                    g.tensor_scalar(diag[:, i, e, :], ident[:, :], Kk[:, k, e:e + 1], 1.0, MUL, MUL
                                    ).then_inc(diag_ready, 1)
            for q in range(2):
                s = slice(3 * q, 3 * q + 3)
                pool.wait_ge(var2, q + 1)
                g.tensor_tensor(rs2[:, s], ve2[:, s], half_exp[0:BH, 0, 0:3], ALU.pow).then_inc(pow2, 1)
            for q in range(2):
                s = slice(3 * q, 3 * q + 3)
                pool.wait_ge(var3, q + 1)
                g.tensor_tensor(rs3[:, :, s], ve3[:, :, s], half_exp[0:BH, :, 0:3], ALU.pow).then_inc(pow3, 1)
            pool.wait_ge(l_bc, 32)
            pool.wait_ge(l_rc, 16)
            g.tensor_tensor(r_tok[0:CT, 4, :], r_tok[0:CT, 4, :], bout_bc[0:CT, :], ADD).then_inc(rtok_ready, 1)
            pool.wait_ge(l_rp, 32)
            for j, (c0, n) in enumerate(PTILES):
                g.tensor_tensor(r_tok[0:n, j, :], r_tok[0:n, j, :], bout_bc[0:n, :], ADD).then_inc(rtok_ready, 1)
            pool.wait_ge(var4, 1)
            g.tensor_tensor(rs4[0:CT, 4:5], ve4[0:CT, 4:5], half_exp[0:CT, 0, 0:1], ALU.pow).then_inc(pow4, 1)
            for j, (c0, n) in enumerate(PTILES):
                pool.wait_ge(var4, j + 2)
                g.tensor_tensor(rs4[0:n, j:j + 1], ve4[0:n, j:j + 1], half_exp[0:n, 0, 0:1], ALU.pow
                                ).then_inc(pow4, 1)
            for j, (c0, n) in enumerate(PTILES):
                g.tensor_tensor(h3b[0:n, j, :], h3[0:n, j, :], m0b2_bc[0:n, :], ADD).then_inc(h3b_ready, 1)

        @block.scalar
        def _(act):
            a_ = nc.scalar
            for i, v in enumerate((A, Bp, C)):
                act.dma_start(ssm[:, i], v.rearrange("(e p) n -> p e n", p=128)).then_inc(l_ssm, 16)
            act.dma_start(cw[:, :, :], conv_w.rearrange("(e p) n -> p e n", p=128)).then_inc(l_ssm, 16)
            act.dma_start(tokb_row[:, :], tok_b.unsqueeze(0)).then_inc(l_tokb, 16)
            act.dma_start(cls_sb[:, :], cls[0].partition_broadcast(NB)).then_inc(l_cls, 16)
            act.dma_start(pos0_sb[:, :], pos[0].partition_broadcast(NB)).then_inc(l_cls, 16)
            act.dma_start(ln2w_bc[:, :], ln2_w.partition_broadcast(BH)).then_inc(l_ln2, 16)
            act.dma_start(ln2b_bc[:, :], ln2_b.partition_broadcast(BH)).then_inc(l_ln2, 16)
            act.dma_start(posb[:, :, :].rearrange("p n d -> p (n d)"),
                          pos[1:T].rearrange("(n w) d -> n (w d)", w=NW).unsqueeze(0).broadcast_to(
                              [NB, NH, NW * D])).then_inc(l_pos, 16)
            act.dma_start(half_rows[0:2 * NEXP, :], A2_b.rearrange("a (h p) -> (a h) p", p=DH)).then_inc(l_half, 16)
            act.dma_start(half_rows[2 * NEXP:, :], gamma.rearrange("(h p) -> h p", p=DH)).then_inc(l_half, 16)
            act.dma_start(bias_rows[0:M0_COL, :], A1_b.rearrange("a (m p) -> (a m) p", p=128)).then_inc(l_rows, 16)
            act.dma_start(bias_rows[M0_COL:W_IN_COL, :], m0_b1.rearrange("(m p) -> m p", p=128)).then_inc(l_rows, 16)
            act.dma_start(bias_rows[W_IN_COL:, :], b_in.rearrange("(m p) -> m p", p=128)).then_inc(l_rows, 16)
            act.dma_start(bout_bc[:, :], b_out.partition_broadcast(128)).then_inc(l_bc, 16)
            act.dma_start(m0b2_bc[:, :], m0_b2.partition_broadcast(128)).then_inc(l_bc, 16)
            act.wait_ge(l_ssm, 64)
            a_.activation(ssm[:, :, :, :], ssm[:, :, :, :], ACT.Sigmoid).then_inc(sig_ready, 1)
            act.wait_ge(t_rows, 1)
            a_.activation(fold_rows[:, :], ps[0:2, 6, 0:D], ACT.Identity).then_inc(rows_ready, 1)
            act.wait_ge(t_fold, 1)
            a_.activation(fold_bc[:, :, :], ps[0:BH, 7, 0:2 * D].rearrange("p (k d) -> p k d", k=2),
                          ACT.Identity).then_inc(fold_ready, 1)
            def line_up(i):
                c, hh = chunks[i]
                act.wait_ge(l_x[c], 16)
                a_.activation(xr[:, i].rearrange("p n (y w) -> p n y w", y=HB),
                              x_pix[:, c, hh * HB:(hh + 1) * HB].rearrange("p y n w -> p n y w"), ACT.Identity
                              ).then_inc(xr_ready, 1)

            for i in range(2):
                line_up(i)
            for i in range(KC):
                b0 = 2 * (i % 2)
                if 0 < i < KC - 1:
                    line_up(i + 1)
                act.wait_ge(t_x, i + 1)
                a_.activation(xT[:, i].rearrange("p (g n) q -> p g (n q)", g=2), ps[:, b0:b0 + 2, 0:3 * BH],
                              ACT.Identity).then_inc(xT_ready, 1)
            act.wait_ge(t_cols, 1)
            a_.activation(bias_col[:, :], ps[:, 7, 0:bias_col.shape[1]], ACT.Identity).then_inc(cols_ready, 1)
            a_.activation(half_col[:, :], ps[0:DH, 7, 64:64 + half_col.shape[1]], ACT.Identity
                          ).then_inc(cols_ready, 1)
            act.wait_ge(cols_ready, 2)
            for hh in range(2):
                act.wait_ge(t_w, hh + 1)
                a_.activation(WinT[:, hh, :], ps[0:DH, hh, 0:E], ACT.Identity,
                              scale=col(half_col, GAMMA_COL + hh)).then_inc(wT_ready, 1)
            act.wait_ge(t_w, 3)
            a_.activation(WoutT[:, 0:2, :], ps[:, 2, 0:2 * D].rearrange("p (e d) -> p e d", e=2),
                          ACT.Identity).then_inc(wT_ready, 1)
            act.wait_ge(t_w, 4)
            a_.activation(WoutT[:, 2, :], ps[:, 3, 0:D], ACT.Identity).then_inc(wT_ready, 1)
            def put_xnT(nw):
                act.wait_ge(t_xs, nw + 2)
                dst = xnT[:, :, :].rearrange("p h (t b) -> p h t b", b=NB)[:, :, 1 + nw:T:NW, :]
                src = ps[0:DH, nw % 4, 0:2 * BH].rearrange("p (h b n) -> p h n b", h=2, n=NH)
                for hh in range(2):
                    a_.activation(dst[:, hh], src[:, hh], ACT.Identity).then_inc(xnT_ready, 1)

            def put_r(nw, n):
                act.wait_ge(rc_ready, 1 if nw == NW else 2 + nw // 3)
                a_.activation(r[0:n, nw, :], h2[0:n, nw, :], ACT.Identity, bias=nm3[0:n, nw:nw + 1],
                              scale=one3[0:n, nw:nw + 1]).then_inc(r_ready, 1)

            put_r(NW, NB)
            act.wait_ge(t_xs, 1)
            a_.activation(xnT[:, :, 0:NB], ps[0:DH, 7, 96:96 + 2 * NB].rearrange("p (h b) -> p h b", h=2),
                          ACT.Identity).then_inc(xnT_ready, 1)
            for nw in range(NW):
                put_xnT(nw)
            for i in range(2 * ET):
                e, c0, c1 = i % ET, (0, SPLIT)[i // ET], (SPLIT, NT)[i // ET]
                act.wait_ge(t_xp, i + 1)
                a_.activation(xp[:, e, c0:c1], ps[:, XP_BANK[i], 0:c1 - c0], ACT.Identity,
                              bias=col(bias_col, W_IN_COL + e)).then_inc(xp_ready, 1)
            for nw in range(NW):
                put_r(nw, BH)
            act.wait_ge(t_x4c, 1)
            a_.activation(x4T[:, :, 0:CT], ps[0:DH, 6, 0:2 * CT].rearrange("p (h t) -> p h t", h=2),
                          ACT.Identity).then_inc(x4T_ready, 1)
            act.wait_ge(gmax_ready, 1)
            a_.activation(g_e[:, :], g_d[:, :], ACT.Exp).then_inc(gexp_ready, 1)
            for q in range(2):
                banks = ((7, 0), (1, 6))[q]
                for m in range(M):
                    src = ps[:, banks[m // 3], (m % 3) * CT:(m % 3 + 1) * CT]
                    act.wait_ge(t_upc, q * M + m - m % 3 + 3)
                    for k in range(3 - q):
                        if q == 0:
                            s_in, s_out_, a = src[:, 32 * k:32 * k + 32], hidc[:, 0, m, 32 * k:32 * k + 32], k
                        else:
                            a = 3 + k
                            s_in = src.rearrange("p (i j b) -> p i j b", j=2, b=NB)[:, :, k]
                            s_out_ = hidc[:, 1, m].rearrange("p (i j b) -> p i j b", j=2, b=NB)[:, :, k]
                        a_.activation(s_out_, s_in, ACT.Gelu, bias=col(bias_col, a * M + m)
                                      ).then_inc(hidc_ready, 1)
            for q in range(2):
                act.wait_ge(t_dnc, q + 1)
                for hh in range(2):
                    src = ps[0:DH, (5, 7)[q], hh * CT:(hh + 1) * CT]
                    for k in range(2 + q):
                        if q == 0:
                            c = 3 + k
                            s_in = src.rearrange("p (i j b) -> p i j b", j=2, b=NB)[:, :, k]
                            s_out_ = oTc[:, 0, hh].rearrange("p (i j b) -> p i j b", j=2, b=NB)[:, :, k]
                        else:
                            c = k
                            s_in, s_out_ = src[:, 32 * k:32 * k + 32], oTc[:, 1, hh, 32 * k:32 * k + 32]
                        a_.activation(s_out_, s_in, ACT.Identity, bias=col(half_col, 2 * c + hh)
                                      ).then_inc(oTc_ready, 1)
            for j, (c0, n) in enumerate(PTILES):
                act.wait_ge(t_x4, j + 1)
                a_.activation(x4T[:, :, CT + c0:CT + c0 + n],
                              ps[0:DH, X4_BANK[j], 0:2 * n].rearrange("p (h t) -> p h t", h=2),
                              ACT.Identity).then_inc(x4T_ready, 1)
                if j % 2 == 0:
                    continue
                c0, n = HALF[j // 2]
                for m in range(M):
                    i = (j // 2) * M + m
                    act.wait_ge(t_up, i + 1)
                    a_.activation(hid[:, m, c0:c0 + n], ps[:, UP_BANK[i % 4], 0:n], ACT.Gelu,
                                  bias=col(bias_col, M0_COL + m)).then_inc(hid_ready, 1)

        @block.vector
        def _(dve):
            v = nc.vector
            n_step = [0]

            def step(ins):
                n_step[0] += 1
                ins.then_inc(vec_step, 1)
                return n_step[0]

            dve.wait_ge(t_ln1, 1)
            v.tensor_copy(ln1_col[:, :, :], ps[:, 7, 0:4 * NC].rearrange("p (c k) -> p c k", c=NC)
                          ).then_inc(ln1c_ready, 1)
            dve.wait_ge(ln1c_ready, 1)
            dve.wait_ge(l_W, 16)
            for c, hh in chunks:
                v.tensor_scalar(Wp[:, hh, c, :], W_sb[:, hh, c, :], ln1_col[:, c, hh:hh + 1], None, MUL
                                ).then_inc(Wp_ready, 1)

            def norm3_coef(p, s, wait_pow):
                dve.wait_ge(*wait_pow)
                k = step(v.tensor_tensor(rms3[0:p, s], rs3[0:p, 0, s], rs3[0:p, 1, s], MUL))
                v.tensor_scalar(one3[0:p, s], rs3[0:p, 0, s], 1.0, None, ADD).then_inc(rc_ready, 0) if False else None
                k1 = step(v.tensor_scalar(one3[0:p, s], rs3[0:p, 0, s], 1.0, None, ADD))
                dve.wait_ge(vec_step, k)
                k = step(v.tensor_scalar(rms3[0:p, s], rms3[0:p, s], EPS6, None, ADD))
                v.scalar_tensor_tensor(nm3[0:p, s], ag3[0:p, s, 0], -1.0, rs3[0:p, 0, s], MUL, MUL
                                       ).then_inc(rc_ready, 1)
                dve.wait_ge(vec_step, k)
                k = step(v.reciprocal(rms3[0:p, s], rms3[0:p, s]))
                dve.wait_ge(vec_step, k)
                k = step(v.tensor_tensor(sc3[0:p, s], rms3[0:p, s], rs3[0:p, 0, s], MUL))
                dve.wait_ge(vec_step, k)

            cn = slice(NW, NW + 1)
            dve.wait_ge(l_cls, 32)
            k = step(v.tensor_tensor(h2[0:NB, NW, :], cls_sb[:, :], pos0_sb[:, :], ADD))
            dve.wait_ge(vec_step, k)
            k = step(v.bn_stats(st3[0:NB, NW, :], h2[0:NB, NW, :]))
            dve.wait_ge(vec_step, k)
            k = step(v.bn_aggr(ag3[0:NB, NW, :], st3[0:NB, NW, :]))
            dve.wait_ge(vec_step, k)
            k = step(v.tensor_scalar(ve3[0:NB, 0, cn], ag3[0:NB, cn, 1], EPS5, None, ADD))
            v.tensor_copy(ve3[0:NB, 1, cn], ag3[0:NB, cn, 1]).then_inc(var0, 1)

            dve.wait_ge(sig_ready, 1)
            sA = ssm[:, 0].rearrange("p e n -> p (e n)")
            k = step(v.tensor_tensor(powr[:, 0, :], ssm[:, 1].rearrange("p e n -> p (e n)"),
                                     ssm[:, 2].rearrange("p e n -> p (e n)"), MUL))
            dve.wait_ge(vec_step, k)
            k = step(v.tensor_tensor(powr[:, 1, :], powr[:, 0, :], sA, MUL))
            base, cur, i = sA, 2, 0
            while cur < T:
                kq = step(v.tensor_tensor(sq[:, i, :], base, base, MUL))
                dve.wait_ge(vec_step, kq)
                base = sq[:, i, :]
                n = min(cur, T - cur)
                k = step(v.tensor_tensor(powr[:, cur:cur + n, :], powr[:, 0:n, :],
                                         base.unsqueeze(1).broadcast_to([128, n, ET * NST]), MUL))
                cur, i = cur + n, i + 1
            dve.wait_ge(vec_step, k)
            k = step(v.tensor_reduce(Gk[:, :, :], powr[:, :, :].rearrange("p k (e n) -> p k e n", e=ET), AX.X, ADD))
            dve.wait_ge(vec_step, k)
            for j in range(DC):
                dst = Kk[:, :, :] if j == 0 else ktmp[:, j, j:T, :]
                k = step(v.tensor_tensor(dst, Gk[:, 0:T - j, :],
                                         cw[:, :, DC - 1 - j].unsqueeze(1).broadcast_to([128, T - j, ET]), MUL))
            dve.wait_ge(vec_step, k)
            for j in range(1, DC):
                ins = v.tensor_tensor(Kk[:, j:T, :], Kk[:, j:T, :], ktmp[:, j, j:T, :], ADD)
                if j < DC - 1:
                    k = step(ins)
                    dve.wait_ge(vec_step, k)
                else:
                    ins.then_inc(K_ready, 1)
            norm3_coef(NB, cn, (pow0, 1))
            v.tensor_scalar(xs[0:NB, NW, :], h2[0:NB, NW, :], ag3[0:NB, NW, 0:1], sc3[0:NB, cn], SUB, MUL
                            ).then_inc(xs_ready, 1)

            for c in range(NC):
                dve.wait_ge(l_x[c], 16)
                for nw in range(NW):
                    k = step(v.bn_stats(st1[:, nw, c, :], x_pix[:, c, :, nw, :]))
            dve.wait_ge(vec_step, k)
            for nw in range(NW):
                k = step(v.bn_aggr(ag1[:, nw, :], st1[:, nw].rearrange("p c s -> p (c s)")))
            dve.wait_ge(vec_step, k)
            v.tensor_scalar(ve1[:, :], ag1[:, :, 1], EPS5, None, ADD).then_inc(var1, 1)
            dve.wait_ge(pow1, 1)
            k = step(v.scalar_tensor_tensor(nm1[:, :], ag1[:, :, 0], -1.0, rs1[:, :], MUL, MUL))
            dve.wait_ge(vec_step, k)
            dve.wait_ge(fold_ready, 1)
            for nw in range(NW):
                k = step(v.scalar_tensor_tensor(ub[:, nw, :], fold_bc[:, 0, :], nm1[:, nw:nw + 1], fold_bc[:, 1, :],
                                                MUL, ADD))
            dve.wait_ge(vec_step, k)

            for q in range(2):
                nws = range(3 * q, 3 * q + 3)
                s = slice(3 * q, 3 * q + 3)
                for nw in nws:
                    dve.wait_ge(t_h, nw + 2 - nw % 2)
                    v.scalar_tensor_tensor(h[:, nw, :], hbank(nw), rs1[:, nw:nw + 1], ub[:, nw, :], MUL, ADD
                                           ).then_inc(h_read, 1)
                for nw in nws:
                    dve.wait_ge(h_read, nw + 1)
                    k = step(v.bn_stats(st2[:, nw, :], h[:, nw, :]))
                dve.wait_ge(vec_step, k)
                for nw in nws:
                    k = step(v.bn_aggr(ag2[:, nw, :], st2[:, nw, :]))
                dve.wait_ge(vec_step, k)
                v.tensor_scalar(ve2[:, s], ag2[:, s, 1], EPS5, None, ADD).then_inc(var2, 1)
            dve.wait_ge(posb_ready, 1)
            for q in range(2):
                nws = range(3 * q, 3 * q + 3)
                s = slice(3 * q, 3 * q + 3)
                for nw in nws:
                    k = step(v.scalar_tensor_tensor(h[:, nw, :], h[:, nw, :], ag2[:, nw, 0:1], ln2w_bc[:, :],
                                                    SUB, MUL))
                dve.wait_ge(vec_step, k)
                dve.wait_ge(pow2, q + 1)
                for nw in nws:
                    k = step(v.scalar_tensor_tensor(h2[:, nw, :], h[:, nw, :], rs2[:, nw:nw + 1], posb[:, nw, :],
                                                    MUL, ADD))
                dve.wait_ge(vec_step, k)
                for nw in nws:
                    k = step(v.bn_stats(st3[:, nw, :], h2[:, nw, :]))
                dve.wait_ge(vec_step, k)
                for nw in nws:
                    k = step(v.bn_aggr(ag3[:, nw, :], st3[:, nw, :]))
                dve.wait_ge(vec_step, k)
                k = step(v.tensor_scalar(ve3[:, 0, s], ag3[:, s, 1], EPS5, None, ADD))
                v.tensor_copy(ve3[:, 1, s], ag3[:, s, 1]).then_inc(var3, 1)
            for q in range(2):
                norm3_coef(BH, slice(3 * q, 3 * q + 3), (pow3, q + 1))
                for nw in range(3 * q, 3 * q + 3):
                    v.tensor_scalar(xs[:, nw, :], h2[:, nw, :], ag3[:, nw, 0:1], sc3[:, nw:nw + 1], SUB, MUL
                                    ).then_inc(xs_ready, 1)

            last = [0] * ET

            def tap(e, k, c0, c1, first):
                lo = max(c0, k * NB)
                dst, src = y[:, e, lo:c1], xp[:, e, lo - k * NB:c1 - k * NB]
                if first:
                    return v.tensor_scalar(dst, src, Kk[:, k, e:e + 1], None, MUL)
                dve.wait_ge(vec_step, last[e])
                return v.scalar_tensor_tensor(dst, src, Kk[:, k, e:e + 1], dst, MUL, ADD)

            for k in range(NCLS):
                for e in range(ET):
                    if k == 0:
                        dve.wait_ge(xp_ready, e + 1)
                    ins = tap(e, k, 0, CT, k == 0)
                    if k < NCLS - 1:
                        last[e] = step(ins)
                    else:
                        ins.then_inc(ycls_ready, 1)

            todo = list(VE_TAPS)

            def taps(n):
                for _ in range(min(n, len(todo))):
                    k = todo.pop(0)
                    for e in range(ET):
                        if k == VE_TAPS[0]:
                            dve.wait_ge(xp_ready, ET + e + 1)
                        last[e] = step(tap(e, k, CT, NT, k == VE_TAPS[0]))

            def norm4(j, n, bank, col0):
                dve.wait_ge(*((t_woc, 1) if j == 4 else (t_wo, j + 1)))
                dve.wait_ge(rtok_ready, 1 if j == 4 else j + 2)
                v.tensor_tensor(h3[0:n, j, :], ps[0:n, bank, 0:D], r_tok[0:n, j, :], ADD).then_inc(h3_ready, 1)
                dve.wait_ge(h3_ready, 1 if j == 4 else j + 2)
                k = step(v.bn_stats(st4[0:n, j, :], h3[0:n, j, :]))
                dve.wait_ge(vec_step, k)
                k = step(v.bn_aggr(ag4[0:n, j, :], st4[0:n, j, :]))
                dve.wait_ge(vec_step, k)
                v.tensor_scalar(ve4[0:n, j:j + 1], ag4[0:n, j, 1:2], EPS5, None, ADD).then_inc(var4, 1)

            def apply4(j, n):
                dve.wait_ge(pow4, 1 if j == 4 else j + 2)
                v.tensor_scalar(x4[0:n, j, :], h3[0:n, j, :], ag4[0:n, j, 0:1], rs4[0:n, j:j + 1], SUB, MUL
                                ).then_inc(x4_ready, 1)

            taps(VE_PARTS[0])
            k = step(v.tensor_reduce(cmask[:, :], ident[0:CT, 0:CT].rearrange("p (i b) -> p i b", b=NB), AX.X, ADD))
            norm4(4, CT, 5, 0)
            taps(VE_PARTS[1])
            apply4(4, CT)
            taps(VE_PARTS[2])
            dve.wait_ge(t_g, 1)
            k = step(v.tensor_tensor(gsel[:, :, :], ps[0:CT, 5, 0:2 * NCLS].rearrange("p (i j) -> p i j", j=2),
                                     cmask[:, :].unsqueeze(2).broadcast_to([CT, NCLS, 2]), MUL))
            dve.wait_ge(vec_step, k)
            k = step(v.tensor_reduce(lg[:, :], gsel[:, :, :].rearrange("p i j -> p j i"), AX.X, ADD))
            dve.wait_ge(vec_step, k)
            k = step(v.tensor_reduce(g_mx[:, :], lg[:, :], AX.X, ALU.max))
            dve.wait_ge(vec_step, k)
            v.tensor_scalar(g_d[:, :], lg[:, :], g_mx[:, 0:1], None, SUB).then_inc(gmax_ready, 1)
            taps(VE_PARTS[3])
            dve.wait_ge(gexp_ready, 1)
            k = step(v.tensor_reduce(g_s[:, :], g_e[:, :], AX.X, ADD))
            dve.wait_ge(vec_step, k)
            k = step(v.reciprocal(g_s[:, :], g_s[:, :]))
            dve.wait_ge(vec_step, k)
            k = step(v.tensor_scalar(g_p[:, :], g_e[:, :], g_s[:, 0:1], None, MUL))
            dve.wait_ge(vec_step, k)
            k = step(v.tensor_reduce(g_mx[:, :], g_p[:, :], AX.X, ALU.min))
            dve.wait_ge(vec_step, k)
            k = step(v.tensor_scalar(g_m[:, :], g_p[:, :], g_mx[:, 0:1], None, ALU.is_gt))
            dve.wait_ge(vec_step, k)
            k = step(v.tensor_tensor(g_p[:, :], g_p[:, :], g_m[:, :], MUL))
            dve.wait_ge(vec_step, k)
            k = step(v.tensor_reduce(g_s[:, :], g_p[:, :], AX.X, ADD))
            dve.wait_ge(vec_step, k)
            k = step(v.tensor_scalar(g_s[:, :], g_s[:, :], EPS6, None, ALU.max))
            dve.wait_ge(vec_step, k)
            k = step(v.reciprocal(g_s[:, :], g_s[:, :]))
            dve.wait_ge(vec_step, k)
            k = step(v.tensor_scalar(gate[:, :], g_p[:, :], g_s[:, 0:1], None, MUL))
            dve.wait_ge(vec_step, k)
            taps(VE_PARTS[4])
            dve.wait_ge(t_oc, 1)
            k = step(v.scalar_tensor_tensor(oc1[:, :], ps[0:CT, 0, 0:D], gate[:, 0:1], h3[0:CT, 4, :], MUL, ADD))
            dve.wait_ge(vec_step, k)
            v.scalar_tensor_tensor(oc[:, :], ps[0:CT, 0, D:2 * D], gate[:, 1:2], oc1[:, :], MUL, ADD
                                   ).then_inc(oc_ready, 1)
            taps(len(todo))
            for c0, n in HALF:
                for e in range(ET):
                    dve.wait_ge(t_y, e + 1)
                    dve.wait_ge(vec_step, last[e])
                    dst = y[:, e, CT + c0:CT + c0 + n]
                    v.tensor_tensor(dst, ps[:, Y_BANK[e], c0:c0 + n], dst, ADD).then_inc(y_ready, 1)
            for q in range(2):
                for j in (2 * q, 2 * q + 1):
                    norm4(j, PTILES[j][1], WO_BANK[j], 0)
                for j in (2 * q, 2 * q + 1):
                    apply4(j, PTILES[j][1])
            for j, (c0, n) in enumerate(PTILES):
                dve.wait_ge(t_dn, j + 1)
                dve.wait_ge(h3b_ready, j + 1)
                v.tensor_tensor(o[0:n, j, :], ps[0:n, WO_BANK[j], 0:D], h3b[0:n, j, :], ADD).then_inc(o_ready, 1)

        @block.tensor
        def _(pe):
            t = nc.tensor

            def mm(out_, lhsT, rhs, start, stop):
                return t.matmul(out_, lhsT, rhs, start=start, stop=stop, skip_group_check=True)

            pe.wait_ge(ident_ready, 1)
            pe.wait_ge(l_ln1, 32)
            rows = ln1_rows[:, :].rearrange("k (p c) -> k c p", c=NC)
            for c in range(NC):
                ins = t.transpose(ps[:, 7, 4 * c:4 * c + 4], rows[:, c, :], ident[0:4, 0:4])
            ins.then_inc(t_ln1, 1)
            pe.wait_ge(ln1c_ready, 1)
            pe.wait_ge(l_W, 16)
            for i, (c, hh) in enumerate(chunks):
                mm(ps[0:2, 6, 0:D], ln1_col[:, c, hh:4:2], W_sb[:, hh, c, :], i == 0, False)
            pe.wait_ge(const_ready, 6)
            pe.wait_ge(l_tokb, 16)
            mm(ps[0:2, 6, 0:D], sel01[:, :], tokb_row[:, :], False, True).then_inc(t_rows, 1)
            pe.wait_ge(rows_ready, 1)
            for i in range(2):
                ins = mm(ps[0:BH, 7, i * D:(i + 1) * D], sel_rows[:, i, 0:BH], fold_rows[:, :], i == 0, True)
            ins.then_inc(t_fold, 1)

            def product(i):
                c, hh = chunks[i]
                pe.wait_ge(xT_ready, i + 1)
                pe.wait_ge(Wp_ready, i + 1)
                for nw in range(NW):
                    ins = mm(hbank(nw), xT[:, i, nw, :], Wp[:, hh, c, :], i == 0 and nw % 2 == 0, i == KC - 1)
                    if i == KC - 1:
                        ins.then_inc(t_h, 1)

            for i, (c, hh) in enumerate(chunks):
                pe.wait_ge(xr_ready, i + 1)
                if i >= 2:
                    pe.wait_ge(xT_ready, i - 1)
                for nw in range(NW):
                    ins = t.transpose(ps[:, 2 * (i % 2) + nw // 3, (nw % 3) * BH:(nw % 3 + 1) * BH],
                                      xr[:, i, nw, :], ident[0:BH, 0:BH])
                ins.then_inc(t_x, 1)
                if i >= 1:
                    product(i - 1)
            product(KC - 1)

            pe.wait_ge(fold_ready, 1)
            pe.wait_ge(l_rows, 48)
            nr, nhr = bias_rows.shape[0], half_rows.shape[0]
            t.transpose(ps[:, 7, 0:nr], bias_rows[:, :], ident[0:nr, 0:nr])
            pe.wait_ge(l_half, 32)
            t.transpose(ps[0:DH, 7, 64:64 + nhr], half_rows[:, :], ident[0:nhr, 0:nhr]).then_inc(t_cols, 1)
            pe.wait_ge(xT_ready, KC)
            pe.wait_ge(l_Win, 16)
            for hh in range(2):
                for e in range(ET):
                    ins = t.transpose(ps[0:DH, hh, e * 128:(e + 1) * 128], Win_sb[:, e, hh * DH:(hh + 1) * DH],
                                      ident[:, :])
                ins.then_inc(t_w, 1)
            pe.wait_ge(l_Wout, 16)
            for e in range(ET):
                for hh in range(2):
                    c0 = (e % 2) * D + hh * DH
                    ins = t.transpose(ps[:, 2 + e // 2, c0:c0 + DH], Wout_sb[:, hh, e * 128:(e + 1) * 128],
                                      ident[0:DH, 0:DH])
                if e >= 1:
                    ins.then_inc(t_w, 1)

            pe.wait_ge(cols_ready, 2)
            pe.wait_ge(xs_ready, 1)
            for hh in range(2):
                ins = t.transpose(ps[0:DH, 7, 96 + hh * NB:96 + (hh + 1) * NB], xs[0:NB, NW, hh * DH:(hh + 1) * DH],
                                  ident[0:NB, 0:NB])
            ins.then_inc(t_xs, 1)
            for nw in range(NW):
                pe.wait_ge(xs_ready, nw + 2)
                if nw < 4:
                    pe.wait_ge(wT_ready, (1, 2, 3, 4)[nw])
                else:
                    pe.wait_ge(xnT_ready, 1 + 2 * (nw - 3))
                for hh in range(2):
                    ins = t.transpose(ps[0:DH, nw % 4, hh * BH:(hh + 1) * BH], xs[:, nw, hh * DH:(hh + 1) * DH],
                                      ident[0:BH, 0:BH])
                ins.then_inc(t_xs, 1)
            pe.wait_ge(h_read, NW)
            pe.wait_ge(xnT_ready, 1 + 2 * NW)
            for i in range(2 * ET):
                e, c0, c1 = i % ET, (0, SPLIT)[i // ET], (SPLIT, NT)[i // ET]
                for hh in range(2):
                    ins = mm(ps[:, XP_BANK[i], 0:c1 - c0], WinT[:, hh, e * 128:(e + 1) * 128], xnT[:, hh, c0:c1],
                             hh == 0, hh == 1)
                ins.then_inc(t_xp, 1)

            todo = list(range(NDG))

            def taps(n):
                for _ in range(min(n, len(todo))):
                    i = todo.pop(0)
                    k = PE_TAPS[i]
                    lo = max(CT, k * NB)
                    for e in range(ET):
                        if i == 0:
                            pe.wait_ge(xp_ready, ET + e + 1)
                        pe.wait_ge(diag_ready, i * ET + e + 1)
                        ins = mm(ps[:, Y_BANK[e], lo - CT:PT], diag[:, i, e, :], xp[:, e, lo - k * NB:NT - k * NB],
                                 i == 0, i == NDG - 1)
                        if i == NDG - 1:
                            ins.then_inc(t_y, 1)

            def project(cols, n, bank, done):
                for e in range(ET):
                    ins = mm(ps[0:n, bank, 0:D], y[:, e, cols:cols + n], WoutT[:, e, :], e == 0, e == ET - 1)
                ins.then_inc(done, 1)

            taps(PE_PARTS[0])
            pe.wait_ge(ycls_ready, ET)
            pe.wait_ge(wT_ready, 4)
            project(0, CT, 5, t_woc)
            taps(PE_PARTS[1])
            pe.wait_ge(x4_ready, 1)
            for hh in range(2):
                ins = t.transpose(ps[0:DH, 6, hh * CT:(hh + 1) * CT], x4[0:CT, 4, hh * DH:(hh + 1) * DH],
                                  ident[0:CT, 0:CT])
            ins.then_inc(t_x4c, 1)
            taps(PE_PARTS[2])
            pe.wait_ge(x4T_ready, 1)
            pe.wait_ge(l_G, 32)
            for hh in range(2):
                ins = mm(ps[0:CT, 5, 0:2 * NCLS], x4T[:, hh, 0:CT], G_sb[:, hh].rearrange("p i j -> p (i j)"),
                         hh == 0, hh == 1)
            ins.then_inc(t_g, 1)
            pe.wait_ge(l_A1, 16 * NEXP)
            xc = [x4T[:, hh, 0:CT] for hh in range(2)]
            for q in range(2):
                banks = ((7, 0), (1, 6))[q]
                for m in range(M):
                    dst = ps[:, banks[m // 3], (m % 3) * CT:(m % 3 + 1) * CT]
                    for k in range(3 - q):
                        for hh in range(2):
                            if q == 0:
                                a, d_, s_ = k, dst[:, 32 * k:32 * k + 32], xc[hh][:, 32 * k:32 * k + 32]
                            else:
                                a = 3 + k
                                d_ = dst.rearrange("p (i j b) -> p i j b", j=2, b=NB)[:, :, k]
                                s_ = xc[hh].rearrange("p (i j b) -> p i j b", j=2, b=NB)[:, :, k]
                            ins = mm(d_, A1_sb[:, a, hh, m * 128:(m + 1) * 128], s_, hh == 0, hh == 1)
                    ins.then_inc(t_upc, 1)
            taps(PE_PARTS[3])
            pe.wait_ge(l_A2, 16 * NEXP)
            for q in range(2):
                pe.wait_ge(hidc_ready, (3 * M, 5 * M)[q])
                for hh in range(2):
                    dst = ps[0:DH, (5, 7)[q], hh * CT:(hh + 1) * CT]
                    for k in range(2 + q):
                        for m in range(M):
                            if q == 0:
                                c = 3 + k
                                d_ = dst.rearrange("p (i j b) -> p i j b", j=2, b=NB)[:, :, k]
                                s_ = hidc[:, 0, m].rearrange("p (i j b) -> p i j b", j=2, b=NB)[:, :, k]
                            else:
                                c, d_, s_ = k, dst[:, 32 * k:32 * k + 32], hidc[:, 1, m, 32 * k:32 * k + 32]
                            ins = mm(d_, A2_sb[:, c, m, hh * DH:(hh + 1) * DH], s_, m == 0, m == M - 1)
                ins.then_inc(t_dnc, 1)
            pe.wait_ge(oTc_ready, 10)
            for q in range(2):
                for hh in range(2):
                    c0 = q * D + hh * DH
                    ins = t.transpose(ps[0:CT, 0, c0:c0 + DH], oTc[:, q, hh, :], ident[0:DH, 0:DH])
            ins.then_inc(t_oc, 1)
            taps(len(todo))

            for j, (c0, n) in enumerate(PTILES):
                pe.wait_ge(y_ready, ET * (1 + j // 2))
                project(CT + c0, n, WO_BANK[j], t_wo)
            pe.wait_ge(l_W1, 16)
            for q, (h0, hn) in enumerate(HALF):
                for j in (2 * q, 2 * q + 1):
                    n = PTILES[j][1]
                    pe.wait_ge(x4_ready, j + 2)
                    if q == 1:
                        pe.wait_ge(hid_ready, j + 1)
                    for hh in range(2):
                        ins = t.transpose(ps[0:DH, X4_BANK[j], hh * n:(hh + 1) * n],
                                          x4[0:n, j, hh * DH:(hh + 1) * DH], ident[0:n, 0:n])
                    ins.then_inc(t_x4, 1)
                pe.wait_ge(x4T_ready, 1 + 2 * (q + 1))
                for m in range(M):
                    i = q * M + m
                    if i >= 4:
                        pe.wait_ge(hid_ready, i - 3)
                    elif UP_BANK[i] == 0:
                        pe.wait_ge(oc_ready, 1)
                    for hh in range(2):
                        ins = mm(ps[:, UP_BANK[i % 4], 0:hn], W1_sb[:, hh, m * 128:(m + 1) * 128],
                                 x4T[:, hh, CT + h0:CT + h0 + hn], hh == 0, hh == 1)
                    ins.then_inc(t_up, 1)
            pe.wait_ge(l_W2, 16)
            for j, (c0, n) in enumerate(PTILES):
                for m in range(M):
                    pe.wait_ge(hid_ready, (j // 2) * M + m + 1)
                    ins = mm(ps[0:n, WO_BANK[j], 0:D], hid[:, m, c0:c0 + n], W2_sb[:, m, :], m == 0, m == M - 1)
                ins.then_inc(t_dn, 1)


_INS = ['x', 'L0_tok_ln1_w', 'L0_tok_ln1_b', 'L0_tok_W', 'L0_tok_b', 'L0_tok_ln2_w', 'L0_tok_ln2_b',
        'L0_tok_cls', 'L0_tok_pos', 'L0_attn_gamma', 'L0_attn_W_in', 'L0_attn_b_in', 'L0_attn_conv_w',
        'L0_attn_A', 'L0_attn_Bp', 'L0_attn_C', 'L0_attn_W_out', 'L0_attn_b_out', 'L0_ffn_moe0_W1',
        'L0_ffn_moe0_b1', 'L0_ffn_moe0_W2', 'L0_ffn_moe0_b2', 'L0_ffn_A1_W', 'L0_ffn_A1_b', 'L0_ffn_A2_W',
        'L0_ffn_A2_b', 'L0_ffn_G_W']


def kernel(**inputs):
    import numpy as _np
    import concourse.bacc as _bacc
    from concourse import mybir as _mybir
    from concourse.bass_utils import run_bass_kernel_spmd as _run

    nc = _bacc.Bacc("TRN2", target_bir_lowering=False, num_devices=1)
    arrays, args = {}, []
    for name in _INS:
        a = _np.ascontiguousarray(inputs[name])
        arrays[f"in_{name}_dram"] = a
        args.append(nc.dram_tensor(f"in_{name}_dram", a.shape, _mybir.dt.from_np(a.dtype), kind="ExternalInput").ap())
    shape = (inputs['x'].shape[0], 37, 192)
    args.append(nc.dram_tensor("out_0_dram", shape, _mybir.dt.float32, kind="ExternalOutput").ap())
    vit_tower_kernel(nc, *args)
    res = _run(nc, [arrays], core_ids=[0])
    return res.results[0]["out_0_dram"]
```

```python
import concourse.bass as bass
from concourse import mybir
from contextlib import ExitStack


def vit_tower_kernel(nc, x, ln1_w, ln1_b, tok_W, tok_b, ln2_w, ln2_b, cls, pos,
                     gamma, W_in, b_in, conv_w, A, Bp, C, W_out, b_out,
                     m0_W1, m0_b1, m0_W2, m0_b2, A1_W, A1_b, A2_W, A2_b, G_W, out):
    F32 = mybir.dt.float32
    ALU = mybir.AluOpType
    ACT = mybir.ActivationFunctionType
    AX = mybir.AxisListType
    MUL, ADD, SUB = ALU.mult, ALU.add, ALU.subtract

    NB, NC, IMG, _ = x.shape
    P = 16
    NH = NW = IMG // P
    BH = NB * NH
    D = tok_W.shape[1]
    DH = D // 2
    T = NH * NW + 1
    NT = NB * T
    E = W_in.shape[0]
    ET = E // 128
    NST = A.shape[1]
    DC = conv_w.shape[1]
    NCLS = 6
    CT = NCLS * NB
    PT = NT - CT
    HID = m0_W1.shape[1]
    M = HID // 128
    NEXP = A1_W.shape[0]
    HB = 8
    H2 = P // HB
    KC = NC * H2
    EPS5, EPS6 = 1e-5, 1e-6
    SPLIT = 19 * NB
    PTILES = [(0, 128), (128, 128), (256, 128), (384, PT - 384)]
    HALF = [(0, 256), (256, PT - 256)]
    NLO, NHI = 3, 2
    PE_TAPS = [0, 2, 4, 7, 9, 12, 14, 17, 19, 22, 25, 28, 31, 34]
    PE_PARTS = [4, 3, 1, 1, 1, 1, 1]
    VE_TAPS = [k for k in range(T) if k not in PE_TAPS]
    VE_PARTS = [4, 2, 2, 6, 3]
    assert PE_TAPS[0] * NB <= CT and VE_TAPS[0] * NB <= CT
    NDG = len(PE_TAPS)
    WARM = 14

    ctx = ExitStack()
    with ctx:
        def sb(name, shape):
            return ctx.enter_context(nc.sbuf_tensor(name, shape, F32))

        def within(area, offset, shape):
            n = 1
            for d in shape[1:]:
                n *= d
            v = area[0:shape[0], offset:offset + n]
            if len(shape) > 2:
                names = "abcd"[:len(shape) - 1]
                v = v.rearrange(f"p ({' '.join(names)}) -> p {' '.join(names)}",
                                **{k: d for k, d in zip(names[1:], shape[2:])})
            return v

        def sem(name):
            return ctx.enter_context(nc.semaphore(name))

        ident = sb("ident", [128, 128])
        ones = sb("ones", [1, 64])
        sel01 = sb("sel01", [1, 2])
        eps5 = sb("eps5", [128, 1])
        neg_half = sb("neg_half", [128, 2])
        pixel_area = sb("pixel_area", [128, NC * P * IMG])
        x_sb = within(pixel_area, 0, [BH, NC, P * IMG])
        hid = within(pixel_area, 0, [128, M, PT])
        hid_lo = within(pixel_area, M * PT, [CT, HID])
        hid_hi = within(pixel_area, M * PT + HID, [128, HID])
        line_area = sb("line_area", [128, NEXP * M * D])
        xr = within(line_area, 0, [BH, KC, NW, 128])
        A2_sb = within(line_area, 0, [128, NEXP, M, D])
        xT_area = sb("xT_area", [128, KC * NW * BH])
        xT = within(xT_area, 0, [128, KC, NW, BH])
        h3 = within(xT_area, 0, [128, 5, D])
        h3b = within(xT_area, 5 * D, [128, 5, D])
        x4 = within(xT_area, 10 * D, [128, 5, D])
        hid_cls = within(xT_area, 15 * D, [128, M, CT])
        diag_area = sb("diag_area", [128, NDG * ET * 128])
        powr = within(diag_area, 0, [128, T, ET * NST])
        diag = within(diag_area, 0, [128, NDG, ET, 128])
        xp = sb("xp", [128, ET, NT])
        tok_area = sb("tok_area", [128, ET * NT])
        h = within(tok_area, 0, [BH, NW, D])
        y = within(tok_area, 0, [128, ET, NT])
        Wp_area = sb("Wp_area", [128, KC * D])
        Wp = within(Wp_area, 0, [128, H2, NC, D])
        o = within(Wp_area, 0, [128, 4, D])
        W_area = sb("W_area", [128, KC * D])
        W_sb = within(W_area, 0, [128, H2, NC, D])
        W2_sb = within(W_area, 0, [128, M, D])
        ln1_col = sb("ln1_col", [128, 2, H2, NC])
        tokb_row = sb("tokb_row", [1, D])
        fold_rows = sb("fold_rows", [2, D])
        gamma_col = sb("gamma_col", [DH, 2])
        A2b_row = sb("A2b_row", [1, NEXP, D])
        ssm = sb("ssm", [128, 3, ET, NST])
        cw = sb("cw", [128, ET, DC])
        sq = sb("sq", [128, 6, ET * NST])
        Gk = sb("Gk", [128, T, ET])
        Kk = sb("Kk", [128, T, ET])
        ktmp = sb("ktmp", [128, DC, T, ET])
        ln2w_bc = sb("ln2w_bc", [BH, D])
        ln2b_bc = sb("ln2b_bc", [BH, D])
        posb = sb("posb", [BH, NW, D])
        bout_bc = sb("bout_bc", [128, D])
        m0b2_bc = sb("m0b2_bc", [128, D])
        cls_sb = sb("cls_sb", [NB, D])
        pos0_sb = sb("pos0_sb", [NB, D])
        st1 = sb("st1", [BH, NW, NC, 6])
        ag1 = sb("ag1", [BH, NW, 2])
        ve1 = sb("ve1", [BH, NW])
        ms1 = sb("ms1", [BH, NW, 2])
        ms1T = sb("ms1T", [2, NW, BH])
        st2 = sb("st2", [BH, NW, 6])
        ag2 = sb("ag2", [BH, NW, 2])
        ve2 = sb("ve2", [BH, NW])
        rs2 = sb("rs2", [BH, NW])
        h2 = sb("h2", [BH, NW + 1, D])
        st3 = sb("st3", [BH, NW + 1, 6])
        ag3 = sb("ag3", [BH, NW + 1, 2])
        s3 = sb("s3", [BH, 2, NW + 1])
        one3 = sb("one3", [BH, NW + 1])
        nm3 = sb("nm3", [BH, NW + 1])
        xs = sb("xs", [BH, NW + 1, D])
        r = sb("r", [BH, NW + 1, D])
        Win_sb = sb("Win_sb", [128, ET, D])
        Wout_sb = sb("Wout_sb", [DH, 2, E])
        WinT = sb("WinT", [DH + 1, 2, E])
        WoutT = sb("WoutT", [128, ET, D])
        xnT = sb("xnT", [DH + 1, 2, NT])
        r_tok = sb("r_tok", [128, 5, D])
        st4 = sb("st4", [128, 5, 6])
        ag4 = sb("ag4", [128, 5, 2])
        ve4 = sb("ve4", [128, 5])
        rs4 = sb("rs4", [128, 5])
        x4T = sb("x4T", [DH + 1, 2, NT])
        x_par = sb("x_par", [DH + 1, 2, 2, 64])
        perm = sb("perm", [128, NCLS // 2, 2, NB])
        hid_par = sb("hid_par", [128, M, 2, 64])
        o_par = sb("o_par", [128, D])
        A1_sb = sb("A1_sb", [DH + 1, NEXP, 2, HID])
        W1_sb = sb("W1_sb", [DH + 1, 2, HID])
        G_sb = sb("G_sb", [DH, 2, NCLS, 2])
        cmask = sb("cmask", [CT, NCLS])
        gsel = sb("gsel", [CT, NCLS, 2])
        lg = sb("lg", [CT, 2])
        g_mx = sb("g_mx", [CT, 1])
        g_d = sb("g_d", [CT, 2])
        g_e = sb("g_e", [CT, 2])
        g_s = sb("g_s", [CT, 1])
        g_p = sb("g_p", [CT, 2])
        g_m = sb("g_m", [CT, 2])
        gate = sb("gate", [CT, 2])
        oc1 = sb("oc1", [CT, D])
        oc = sb("oc", [CT, D])
        ps = ctx.enter_context(nc.psum_tensor("ps", [128, 8, 512], F32))
        r_dram = nc.dram_tensor("r_scratch", [NT, D], F32).ap()

        l_ln1, l_ssm, l_cw, l_W, l_tokb, l_cls, l_ln2, l_pos = [sem(f"l_{n}") for n in (
            "ln1", "ssm", "cw", "W", "tokb", "cls", "ln2", "pos")]
        l_x = [sem(f"l_x{c}") for c in range(NC)]
        l_bc, l_Win, l_Wout, l_gamma, l_G, l_A1, l_A2, l_A2b, l_W1, l_W2 = [sem(f"l_{n}") for n in (
            "bc", "Win", "Wout", "gamma", "G", "A1", "A2", "A2b", "W1", "W2")]
        s_rw = sem("s_rw")
        l_rc = sem("l_rc")
        l_rp = sem("l_rp")
        s_out = sem("s_out")
        pool_step = sem("pool_step")
        ident_ready = sem("ident_ready")
        const_ready = sem("const_ready")
        posb_ready = sem("posb_ready")
        perm_ready = sem("perm_ready")
        diag_ready = sem("diag_ready")
        co_ready = sem("co_ready")
        xr5_ready = sem("xr5_ready")
        K_ready = sem("K_ready")
        rtok_ready = sem("rtok_ready")
        rs4_ready = sem("rs4_ready")
        h3b_ready = sem("h3b_ready")
        vec_step = sem("vec_step")
        pads_ready = sem("pads_ready")
        Wp_ready = sem("Wp_ready")
        nm1_ready = sem("nm1_ready")
        var0, var1, var2, var3, var4 = [sem(f"var{i}") for i in range(5)]
        h_read = sem("h_read")
        rc_ready = sem("rc_ready")
        r_ready = sem("r_ready")
        xs_ready = sem("xs_ready")
        ycls_ready = sem("ycls_ready")
        y_ready = sem("y_ready")
        h3_ready = sem("h3_ready")
        x4_ready = sem("x4_ready")
        gmax_ready = sem("gmax_ready")
        oc_ready = sem("oc_ready")
        o_ready = sem("o_ready")
        sig_ready, rows_ready, ms1T_ready, xr_ready, xT_ready, wT_ready = [sem(n) for n in (
            "sig_ready", "rows_ready", "ms1T_ready", "xr_ready", "xT_ready", "wT_ready")]
        rs0_ready, rs1_ready, rs2_ready, rs3_ready = [sem(f"rs{i}_ready") for i in range(4)]
        xnT_ready, xp_ready, x4T_ready, gexp_ready = [sem(n) for n in (
            "xnT_ready", "xp_ready", "x4T_ready", "gexp_ready")]
        hlo_ready, hhi_ready, hpar_ready, hcls_ready, opar_ready, hid_ready = [sem(n) for n in (
            "hlo_ready", "hhi_ready", "hpar_ready", "hcls_ready", "opar_ready", "hid_ready")]
        t_rows, t_ms1, t_x, t_h, t_w, t_xs, t_xp, t_y, t_woc, t_wo, t_x4c, t_x4, t_g = [sem(f"t_{n}") for n in (
            "rows", "ms1", "x", "h", "w", "xs", "xp", "y", "woc", "wo", "x4c", "x4", "g")]
        t_uplo, t_uphi, t_tlo, t_thi, t_dnpar, t_dncls, t_oc, t_up, t_dn = [sem(f"t_{n}") for n in (
            "uplo", "uphi", "tlo", "thi", "dnpar", "dncls", "oc", "up", "dn")]

        chunks = [(c, hh) for c in range(NC) for hh in range(H2)]
        x_pix = x_sb.rearrange("p c (y n w) -> p c y n w", y=P, n=NW)
        WO_BANK = [6, 1, 5, 7]
        X4_BANK = [2, 3, 4, 0]
        UP_BANK = [2, 3, 4, 0]
        Y_BANK = [2, 3, 4]
        XP_BANK = [2, 3, 7, 4, 5, 2, 6, 3, 7]
        XP_DONE = [NW * ET + ET - 2 * (ET - 1 - e) for e in range(ET)]
        NPAIR = NW // 2
        KH = [DH + 1, DH]
        HH = HID // 2
        M2 = M // 2

        def hbank(nw):
            return ps[0:BH, 4 + nw // 2, (nw % 2) * D:(nw % 2 + 1) * D]

        def pair(q):
            return [2 * q, 2 * q + 1]

        def xn_cols(q):
            return (0 if q == 0 else NB + 2 * q * BH), NB + 2 * (q + 1) * BH

        block = ctx.enter_context(nc.Block())

        @block.sync
        def _(sp):
            def load_x(c):
                sp.dma_start(x_sb[:, c, :], x[:, c].rearrange("b (n q) w -> b n (q w)", n=NH)).then_inc(l_x[c], 16)

            load_x(0)
            sp.dma_start(W_sb.rearrange("p h c d -> p h (c d)"),
                         tok_W.rearrange("(h p c) d -> p h (c d)", h=H2, c=NC)).then_inc(l_W, 16)
            sp.dma_start(ln1_col[:, 0], ln1_w.rearrange("(h p c) -> p h c", h=H2, c=NC)).then_inc(l_ln1, 16)
            sp.dma_start(ln1_col[:, 1], ln1_b.rearrange("(h p c) -> p h c", h=H2, c=NC)).then_inc(l_ln1, 16)
            load_x(1)
            load_x(2)
            sp.dma_start(ln2w_bc[:, :], ln2_w.partition_broadcast(BH)).then_inc(l_ln2, 16)
            sp.dma_start(ln2b_bc[:, :], ln2_b.partition_broadcast(BH)).then_inc(l_ln2, 16)
            sp.dma_start(posb[:, :, :].rearrange("p n d -> p (n d)"),
                         pos[1:T].rearrange("(n w) d -> n (w d)", w=NW).unsqueeze(0).broadcast_to(
                             [NB, NH, NW * D])).then_inc(l_pos, 16)
            for hh in range(2):
                sp.dma_start(gamma_col[:, hh:hh + 1], gamma[hh * DH:(hh + 1) * DH].unsqueeze(1)).then_inc(l_gamma, 16)
            sp.dma_start(Win_sb[:, :, :], W_in.rearrange("(e p) d -> p e d", p=128)).then_inc(l_Win, 16)
            sp.dma_start(WinT[DH:DH + 1, 0, :], b_in.unsqueeze(0)).then_inc(l_Win, 16)
            sp.dma_start(Wout_sb[:, :, :], W_out.rearrange("(h p) e -> p h e", p=DH)).then_inc(l_Wout, 16)
            for hh in range(2):
                sp.dma_start(G_sb[:, hh], G_W[:, hh * DH:(hh + 1) * DH, :].rearrange("i p j -> p i j")
                             ).then_inc(l_G, 16)
            for a in range(NEXP):
                sp.dma_start(A1_sb[0:DH, a], A1_W[a].rearrange("(h p) f -> p h f", p=DH)).then_inc(l_A1, 16)
            sp.dma_start(A1_sb[DH:DH + 1, :, 0, :], A1_b.unsqueeze(0)).then_inc(l_A1, 16)
            sp.dma_start(A2b_row[:, :, :], A2_b.unsqueeze(0)).then_inc(l_A2b, 16)
            sp.dma_start(bout_bc[:, :], b_out.partition_broadcast(128)).then_inc(l_bc, 16)
            sp.dma_start(m0b2_bc[:, :], m0_b2.partition_broadcast(128)).then_inc(l_bc, 16)
            sp.dma_start(W1_sb[0:DH, :, :], m0_W1.rearrange("(h p) f -> p h f", p=DH)).then_inc(l_W1, 16)
            sp.dma_start(W1_sb[DH:DH + 1, 0, :], m0_b1.unsqueeze(0)).then_inc(l_W1, 16)
            sp.wait_ge(t_x, KC)
            sp.wait_ge(Wp_ready, KC)
            sp.dma_start(W2_sb[:, :, :], m0_W2.rearrange("(m p) d -> p m d", p=128)).then_inc(l_W2, 16)
            for a in range(NEXP):
                sp.dma_start(A2_sb[:, a], A2_W[a].rearrange("(m p) d -> p m d", p=128)).then_inc(l_A2, 16)
            r_rows = r_dram.rearrange("(t b) d -> t b d", b=NB)
            sp.wait_ge(r_ready, 1)
            sp.dma_start(r_rows[0], r[0:NB, NW, :]).then_inc(s_rw, 16)
            for nw in range(NW):
                sp.wait_ge(r_ready, nw + 2)
                sp.dma_start(r_rows[1 + nw:T:NW].rearrange("n b d -> b n d"), r[:, nw, :]).then_inc(s_rw, 16)
            sp.wait_ge(s_rw, 16 * (NW + 1))
            sp.dma_start(r_tok[0:CT, 4, :], r_dram[0:CT]).then_inc(l_rc, 16)
            sp.dma_start(r_tok[:, 0:3, :], r_dram[CT:CT + 384].rearrange("(j p) d -> p j d", p=128)
                         ).then_inc(l_rp, 16)
            sp.dma_start(r_tok[0:PTILES[3][1], 3, :], r_dram[CT + 384:NT]).then_inc(l_rp, 16)
            o_rows = out.rearrange("b t d -> t b d")
            sp.wait_ge(oc_ready, 1)
            sp.dma_start(o_rows[0:NCLS], oc[:, :]).then_inc(s_out, 16)
            for j, (c0, n) in enumerate(PTILES):
                t0 = NCLS + c0 // NB
                sp.wait_ge(o_ready, j + 1)
                sp.dma_start(o_rows[t0:t0 + n // NB], o[0:n, j, :]).then_inc(s_out, 16)
            sp.wait_ge(s_out, 16 * 5)

        @block.gpsimd
        def _(pool):
            g = nc.gpsimd
            n_step = [0]

            def step(ins):
                n_step[0] += 1
                ins.then_inc(pool_step, 1)
                return n_step[0]

            k = step(g.memset(ident[:, :], 0.0))
            pool.wait_ge(pool_step, k)
            g.affine_select(out=ident[:, :], in_=ident[:, :], compare_op=ALU.not_equal, fill=1.0,
                            base=0, pattern=[[-1, 128]], channel_multiplier=1).then_inc(ident_ready, 1)
            g.memset(ones[:, :], 1.0).then_inc(const_ready, 1)
            g.memset(sel01[:, 0:1], 0.0).then_inc(const_ready, 1)
            g.memset(sel01[:, 1:2], 1.0).then_inc(const_ready, 1)
            g.memset(neg_half[:, :], -0.5).then_inc(const_ready, 1)
            g.memset(eps5[:, :], EPS5).then_inc(const_ready, 1)
            for i, v in enumerate((A, Bp, C)):
                pool.dma_start(ssm[:, i], v.rearrange("(e p) n -> p e n", p=128)).then_inc(l_ssm, 16)
            pool.dma_start(tokb_row[:, :], tok_b.unsqueeze(0)).then_inc(l_tokb, 16)
            pool.dma_start(cls_sb[:, :], cls[0].partition_broadcast(NB)).then_inc(l_cls, 16)
            pool.dma_start(pos0_sb[:, :], pos[0].partition_broadcast(NB)).then_inc(l_cls, 16)
            pool.dma_start(cw[:, :, :], conv_w.rearrange("(e p) n -> p e n", p=128)).then_inc(l_cw, 16)
            pool.wait_ge(ident_ready, 1)
            c, hh = chunks[KC - 1]
            pool.wait_ge(l_x[c], 16)
            g.tensor_scalar(xr[:, KC - 1].rearrange("p n (y w) -> p n y w", y=HB),
                            x_pix[:, c, hh * HB:(hh + 1) * HB].rearrange("p y n w -> p n y w"),
                            1.0, 1.0, MUL, MUL).then_inc(xr5_ready, 1)
            pool.wait_ge(l_pos, 16)
            pool.wait_ge(l_ln2, 32)
            g.tensor_tensor(posb[:, :, :], posb[:, :, :], ln2b_bc[:, :].unsqueeze(1).broadcast_to([BH, NW, D]),
                            ADD).then_inc(posb_ready, 1)
            pool.wait_ge(sig_ready, 1)
            sA = ssm[:, 0].rearrange("p e n -> p (e n)")
            k = step(g.tensor_tensor(powr[:, 0, :], ssm[:, 1].rearrange("p e n -> p (e n)"),
                                     ssm[:, 2].rearrange("p e n -> p (e n)"), MUL))
            pool.wait_ge(pool_step, k)
            k = step(g.tensor_tensor(powr[:, 1, :], powr[:, 0, :], sA, MUL))
            base, cur, i = sA, 2, 0
            while cur < T:
                k = step(g.tensor_tensor(sq[:, i, :], base, base, MUL))
                pool.wait_ge(pool_step, k)
                base = sq[:, i, :]
                n = min(cur, T - cur)
                ins = g.tensor_tensor(powr[:, cur:cur + n, :], powr[:, 0:n, :],
                                      base.unsqueeze(1).broadcast_to([128, n, ET * NST]), MUL)
                cur, i = cur + n, i + 1
                k = step(ins)
            pw4 = powr.rearrange("p k (e n) -> p k e n", e=ET)
            n = NST
            while n > 1:
                n //= 2
                pool.wait_ge(pool_step, k)
                dst = Gk[:, :, :].unsqueeze(3) if n == 1 else pw4[:, :, :, 0:n]
                k = step(g.tensor_tensor(dst, pw4[:, :, :, 0:n], pw4[:, :, :, n:2 * n], ADD))
            pool.wait_ge(l_cw, 16)
            pool.wait_ge(pool_step, k)
            for j in range(DC):
                dst = Kk[:, :, :] if j == 0 else ktmp[:, j, j:T, :]
                k = step(g.tensor_tensor(dst, Gk[:, 0:T - j, :],
                                         cw[:, :, DC - 1 - j].unsqueeze(1).broadcast_to([128, T - j, ET]), MUL))
            for j in range(1, DC):
                pool.wait_ge(pool_step, k)
                ins = g.tensor_tensor(Kk[:, j:T, :], Kk[:, j:T, :], ktmp[:, j, j:T, :], ADD)
                if j < DC - 1:
                    k = step(ins)
                else:
                    ins.then_inc(K_ready, 1)
            for j in range(2):
                g.tensor_scalar(perm[:, :, j, :],
                                ident[:, 64 * j:64 * j + CT // 2].rearrange("p (i b) -> p i b", b=NB),
                                1.0, 1.0, MUL, MUL).then_inc(perm_ready, 1)
            def residual_scales(n, s, count):
                pool.wait_ge(rc_ready, count)
                k = step(g.tensor_scalar(nm3[0:n, s], ag3[0:n, s, 0], -1.0, 1.0, MUL, MUL))
                g.tensor_scalar(one3[0:n, s], s3[0:n, 0, s], 1.0, 1.0, MUL, ADD).then_inc(co_ready, 1)
                pool.wait_ge(pool_step, k)
                g.tensor_tensor(nm3[0:n, s], nm3[0:n, s], s3[0:n, 0, s], MUL).then_inc(co_ready, 1)

            pool.wait_ge(K_ready, 1)
            for i, k in enumerate(PE_TAPS):
                for e in range(ET):
                    g.tensor_scalar(diag[:, i, e, :], ident[:, :], Kk[:, k, e:e + 1], 1.0, MUL, MUL
                                    ).then_inc(diag_ready, 1)
                if i == 2:
                    residual_scales(NB, slice(NW, NW + 1), 1)
                    for q in range(NPAIR):
                        residual_scales(BH, slice(2 * q, 2 * q + 2), q + 2)
                if i == 3:
                    pool.wait_ge(l_bc, 32)
                    pool.wait_ge(l_rc, 16)
                    g.tensor_tensor(r_tok[0:CT, 4, :], r_tok[0:CT, 4, :], bout_bc[0:CT, :], ADD
                                    ).then_inc(rtok_ready, 1)
                if i == 6:
                    pool.wait_ge(var4, 1)
                    g.tensor_tensor(rs4[0:CT, 4:5], ve4[0:CT, 4:5], neg_half[0:CT, 0:1], ALU.pow
                                    ).then_inc(rs4_ready, 1)
            pool.wait_ge(l_rp, 32)
            for j, (c0, n) in enumerate(PTILES):
                g.tensor_tensor(r_tok[0:n, j, :], r_tok[0:n, j, :], bout_bc[0:n, :], ADD).then_inc(rtok_ready, 1)
            for q in range(2):
                n = PTILES[2 * q + 1][1]
                pool.wait_ge(var4, 2 * q + 3)
                g.tensor_tensor(rs4[0:128, 2 * q:2 * q + 2], ve4[0:128, 2 * q:2 * q + 2], neg_half[0:128, :],
                                ALU.pow).then_inc(rs4_ready, 1)
            for j, (c0, n) in enumerate(PTILES):
                g.tensor_tensor(h3b[0:n, j, :], h3[0:n, j, :], m0b2_bc[0:n, :], ADD).then_inc(h3b_ready, 1)

        @block.scalar
        def _(act):
            a_ = nc.scalar

            def copy(dst, src, **kw):
                return a_.activation(dst, src, ACT.Identity, **kw)

            def line_up(i):
                c, hh = chunks[i]
                act.wait_ge(l_x[c], 16)
                copy(xr[:, i].rearrange("p n (y w) -> p n y w", y=HB),
                     x_pix[:, c, hh * HB:(hh + 1) * HB].rearrange("p y n w -> p n y w")).then_inc(xr_ready, 1)

            def put_xT(i):
                b0 = 2 * (i % 2)
                act.wait_ge(t_x, i + 1)
                copy(xT[:, i].rearrange("p (g n) q -> p g (n q)", g=2), ps[:, b0:b0 + 2, 0:3 * BH]
                     ).then_inc(xT_ready, 1)

            line_up(0)
            line_up(1)
            put_xT(0)
            line_up(2)
            put_xT(1)
            line_up(3)
            put_xT(2)
            act.wait_ge(l_ssm, 48)
            a_.activation(ssm[:, :, :, :], ssm[:, :, :, :], ACT.Sigmoid).then_inc(sig_ready, 1)
            line_up(4)
            put_xT(3)
            act.wait_ge(t_rows, 1)
            copy(fold_rows[:, :], ps[0:2, 7, 0:D]).then_inc(rows_ready, 1)
            act.wait_ge(const_ready, 5)
            act.wait_ge(var1, 1)
            a_.activation(ms1[:, :, 1], ag1[:, :, 1], ACT.Sqrt, bias=eps5[0:BH, :]).then_inc(rs1_ready, 1)
            put_xT(4)
            put_xT(5)
            act.wait_ge(t_ms1, 1)
            copy(ms1T[:, 0:3, :], ps[0:2, 7, D:D + 3 * BH].rearrange("p (n q) -> p n q", n=3)).then_inc(ms1T_ready, 1)
            copy(ms1T[:, 3:6, :], ps[0:2, 0, 0:3 * BH].rearrange("p (n q) -> p n q", n=3)).then_inc(ms1T_ready, 1)

            def roots2(q):
                s = slice(2 * q, 2 * q + 2)
                act.wait_ge(var2, q + 1)
                a_.activation(rs2[:, s], ve2[:, s], ACT.Sqrt).then_inc(rs2_ready, 1)

            def roots3(n, s, count):
                act.wait_ge(var3, count)
                a_.activation(s3[0:n, 0, s], ag3[0:n, s, 1], ACT.Sqrt, bias=eps5[0:n, :]).then_inc(rs3_ready, 1)
                a_.activation(s3[0:n, 1, s], ag3[0:n, s, 1], ACT.Sqrt).then_inc(rs3_ready, 1)

            def put_r(n, nws, count):
                act.wait_ge(co_ready, 2 * count)
                for nw in nws:
                    copy(r[0:n, nw, :], h2[0:n, nw, :], bias=nm3[0:n, nw:nw + 1], scale=one3[0:n, nw:nw + 1]
                         ).then_inc(r_ready, 1)

            def put_xnT(q):
                act.wait_ge(t_xs, q + 2)
                c0 = NB + 2 * q * BH
                copy(xnT[0:DH, :, c0:c0 + 2 * BH].rearrange("p h (n q) -> p n h q", n=2),
                     ps[0:DH, q % 2, 0:4 * BH].rearrange("p (n h q) -> p n h q", n=2, h=2)).then_inc(xnT_ready, 1)

            def put_xp(q):
                c0, c1 = xn_cols(q)
                n0 = c1 - c0 - 2 * BH
                for e in range(ET):
                    i = q * ET + e
                    act.wait_ge(t_xp, i + 1)
                    if q == 0:
                        copy(xp[:, e, 0:NB], ps[:, XP_BANK[i], 0:NB]).then_inc(xp_ready, 1)
                    for j in range(2):
                        copy(xp[:, e, NB:NT].rearrange("p (h n b) -> p n h b", h=NH, b=NB)[:, 2 * q + j],
                             ps[:, XP_BANK[i], n0 + j * BH:n0 + (j + 1) * BH].rearrange("p (b h) -> p h b", h=NH)
                             ).then_inc(xp_ready, 1)

            roots3(NB, slice(NW, NW + 1), 1)
            roots2(0)
            act.wait_ge(l_gamma, 32)
            for hh in range(2):
                act.wait_ge(t_w, hh + 1)
                copy(WinT[0:DH, hh, :], ps[0:DH, hh, 0:E], scale=gamma_col[:, hh:hh + 1]).then_inc(wT_ready, 1)
            act.wait_ge(t_w, 3)
            copy(WoutT[:, 0:2, :], ps[:, 2, 0:2 * D].rearrange("p (e d) -> p e d", e=2)).then_inc(wT_ready, 1)
            act.wait_ge(t_w, 4)
            copy(WoutT[:, 2, :], ps[:, 3, 0:D]).then_inc(wT_ready, 1)
            roots3(BH, slice(0, 2), 2)
            act.wait_ge(t_xs, 1)
            copy(xnT[0:DH, :, 0:NB], ps[0:DH, 7, 0:2 * NB].rearrange("p (h b) -> p h b", h=2)
                 ).then_inc(xnT_ready, 1)
            roots2(1)
            put_xnT(0)
            roots3(BH, slice(2, 4), 3)
            roots2(2)
            put_xp(0)
            put_xnT(1)
            roots3(BH, slice(4, 6), 4)
            put_xp(1)
            put_xnT(2)
            put_r(NB, [NW], 1)
            put_r(BH, pair(0), 2)
            put_xp(2)
            put_r(BH, pair(1), 3)
            put_r(BH, pair(2), 4)
            act.wait_ge(t_x4c, 1)
            copy(x4T[0:DH, :, 0:CT], ps[0:DH, 6, 0:2 * CT].rearrange("p (h t) -> p h t", h=2)).then_inc(x4T_ready, 1)
            for hh in range(2):
                copy(x_par[0:DH, hh, :, 0:CT // 2].rearrange("p j (i b) -> p j i b", b=NB),
                     ps[0:DH, 6, hh * CT:(hh + 1) * CT].rearrange("p (i j b) -> p j i b", j=2, b=NB)
                     ).then_inc(x4T_ready, 1)
            act.wait_ge(gmax_ready, 1)
            a_.activation(g_e[:, :], g_d[:, :], ACT.Exp).then_inc(gexp_ready, 1)
            act.wait_ge(t_uplo, 1)
            a_.activation(hid_lo.rearrange("p (k f) -> p k f", k=2), ps[0:CT, 0:2, 0:HH], ACT.Gelu
                          ).then_inc(hlo_ready, 1)
            act.wait_ge(t_uphi, 1)
            a_.activation(hid_hi.rearrange("p (k f) -> p k f", k=2), ps[:, 6:8, 0:HH], ACT.Gelu
                          ).then_inc(hhi_ready, 1)
            for q in range(2):
                act.wait_ge(t_tlo, q + 1)
                for j in range(2):
                    copy(hid_par[:, M2 * q:M2 * (q + 1), j, 0:CT // 2].rearrange("p m (i b) -> p m i b", b=NB),
                         ps[:, q, 0:M2 * CT].rearrange("p (m i j b) -> p m i j b", m=M2, j=2, b=NB)[:, :, :, j]
                         ).then_inc(hpar_ready, 1)
            for q in range(2):
                act.wait_ge(t_thi, q + 1)
                for j in range(2):
                    copy(hid_cls[:, M2 * q:M2 * (q + 1)].rearrange("p m (i j b) -> p m i j b", j=2, b=NB)[:, :, :, j],
                         ps[:, 6 + q, 0:M2 * 128].rearrange("p (m j t) -> p m j t", m=M2, j=2)[:, :, j, 0:CT // 2]
                         .rearrange("p m (i b) -> p m i b", b=NB)).then_inc(hcls_ready, 1)
            act.wait_ge(t_dnpar, 1)
            copy(o_par[:, :], ps[:, 5, 0:D]).then_inc(opar_ready, 1)
            for j, (c0, n) in enumerate(PTILES):
                act.wait_ge(t_x4, j + 1)
                copy(x4T[0:DH, :, CT + c0:CT + c0 + n],
                     ps[0:DH, X4_BANK[j], 0:2 * n].rearrange("p (h t) -> p h t", h=2)).then_inc(x4T_ready, 1)
                if j % 2 == 0:
                    continue
                c0, n = HALF[j // 2]
                for m in range(M):
                    i = (j // 2) * M + m
                    act.wait_ge(t_up, i + 1)
                    a_.activation(hid[:, m, c0:c0 + n], ps[:, UP_BANK[i % 4], 0:n], ACT.Gelu).then_inc(hid_ready, 1)

        @block.vector
        def _(dve):
            v = nc.vector
            n_step = [0]

            def step(ins):
                n_step[0] += 1
                ins.then_inc(vec_step, 1)
                return n_step[0]

            v.memset(xnT[DH:DH + 1, 0, :], 1.0).then_inc(pads_ready, 1)
            v.memset(x4T[DH:DH + 1, 0, :], 1.0).then_inc(pads_ready, 1)
            v.memset(x_par[DH:DH + 1, 0, :, :], 1.0).then_inc(pads_ready, 1)
            v.memset(x_par[0:DH, :, :, CT // 2:], 0.0).then_inc(pads_ready, 1)
            v.memset(hid_par[:, :, :, CT // 2:], 0.0).then_inc(pads_ready, 1)
            v.memset(ve4[96:128, 3:4], 1.0).then_inc(pads_ready, 1)

            def norm3_stats(rows, nws):
                for nw in nws:
                    k = step(v.bn_stats(st3[0:rows, nw, :], h2[0:rows, nw, :]))
                dve.wait_ge(vec_step, k)
                for nw in nws:
                    ins = v.bn_aggr(ag3[0:rows, nw, :], st3[0:rows, nw, :])
                ins.then_inc(var3, 1)

            def norm3_apply(rows, nws, count):
                s = slice(nws[0], nws[-1] + 1)
                dve.wait_ge(var3, count)
                dve.wait_ge(rs3_ready, 2 * count)
                k = step(v.scalar_tensor_tensor(s3[0:rows, 1, s], s3[0:rows, 0, s], EPS6, s3[0:rows, 1, s], MUL, ADD))
                dve.wait_ge(vec_step, k)
                v.reciprocal(s3[0:rows, :, s], s3[0:rows, :, s]).then_inc(rc_ready, 1)
                dve.wait_ge(rc_ready, count)
                for nw in nws:
                    v.tensor_scalar(xs[0:rows, nw, :], h2[0:rows, nw, :], ag3[0:rows, nw, 0:1],
                                    s3[0:rows, 1, nw:nw + 1], SUB, MUL).then_inc(xs_ready, 1)

            for c in range(NC):
                dve.wait_ge(l_x[c], 16)
                for nw in range(NW):
                    k = step(v.bn_stats(st1[:, nw, c, :], x_pix[:, c, :, nw, :]))
                if c == 0:
                    dve.wait_ge(l_ln1, 32)
                    dve.wait_ge(l_W, 16)
                    for cc, hh in chunks:
                        v.tensor_scalar(Wp[:, hh, cc, :], W_sb[:, hh, cc, :], ln1_col[:, 0, hh, cc:cc + 1], None, MUL
                                        ).then_inc(Wp_ready, 1)
            dve.wait_ge(vec_step, k)
            for nw in range(NW):
                ins = v.bn_aggr(ag1[:, nw, :], st1[:, nw].rearrange("p c s -> p (c s)"))
            ins.then_inc(var1, 1)
            dve.wait_ge(var1, 1)
            v.tensor_scalar(ms1[:, :, 0], ag1[:, :, 0], -1.0, None, MUL).then_inc(nm1_ready, 1)
            k = step(v.tensor_scalar(ve1[:, :], ag1[:, :, 1], EPS5, EPS5, ADD, MUL))
            dve.wait_ge(l_cls, 32)
            k = step(v.tensor_tensor(h2[0:NB, NW, :], cls_sb[:, :], pos0_sb[:, :], ADD))
            dve.wait_ge(vec_step, k)
            norm3_stats(NB, [NW])

            def token_rows(q):
                dve.wait_ge(t_h, 2 * q + 2)
                for nw in pair(q):
                    k = step(v.bn_stats(st2[:, nw, :], hbank(nw)))
                dve.wait_ge(vec_step, k)
                for nw in pair(q):
                    k = step(v.bn_aggr(ag2[:, nw, :], st2[:, nw, :]))
                s = slice(2 * q, 2 * q + 2)
                dve.wait_ge(vec_step, k)
                v.tensor_tensor(ve2[:, s], ag2[:, s, 1], ve1[:, s], ADD).then_inc(var2, 1)
                if q == 0:
                    dve.wait_ge(l_ln2, 32)
                for nw in pair(q):
                    v.scalar_tensor_tensor(h[:, nw, :], hbank(nw), ag2[:, nw, 0:1], ln2w_bc[:, :],
                                           SUB, MUL).then_inc(h_read, 1)

            def tokens(q):
                s = slice(2 * q, 2 * q + 2)
                dve.wait_ge(rs2_ready, q + 1)
                k = step(v.reciprocal(rs2[:, s], rs2[:, s]))
                if q == 0:
                    dve.wait_ge(posb_ready, 1)
                dve.wait_ge(vec_step, k)
                dve.wait_ge(h_read, 2 * q + 2)
                for nw in pair(q):
                    k = step(v.scalar_tensor_tensor(h2[:, nw, :], h[:, nw, :], rs2[:, nw:nw + 1], posb[:, nw, :],
                                                    MUL, ADD))
                dve.wait_ge(vec_step, k)
                norm3_stats(BH, pair(q))

            token_rows(0)
            norm3_apply(NB, [NW], 1)
            tokens(0)
            token_rows(1)
            norm3_apply(BH, pair(0), 2)
            tokens(1)
            token_rows(2)
            norm3_apply(BH, pair(1), 3)
            tokens(2)
            norm3_apply(BH, pair(2), 4)

            dve.wait_ge(K_ready, 1)

            last = [0] * ET

            def tap(e, k, c0, c1, first):
                lo = max(c0, k * NB)
                dst, src = y[:, e, lo:c1], xp[:, e, lo - k * NB:c1 - k * NB]
                if first:
                    return v.tensor_scalar(dst, src, Kk[:, k, e:e + 1], None, MUL)
                dve.wait_ge(vec_step, last[e])
                return v.scalar_tensor_tensor(dst, src, Kk[:, k, e:e + 1], dst, MUL, ADD)

            for k in range(NCLS):
                for e in range(ET):
                    if k == 0:
                        dve.wait_ge(xp_ready, XP_DONE[e])
                    ins = tap(e, k, 0, CT, k == 0)
                    if k < NCLS - 1:
                        last[e] = step(ins)
                    else:
                        ins.then_inc(ycls_ready, 1)

            todo = list(VE_TAPS)

            def taps(n):
                for _ in range(min(n, len(todo))):
                    k = todo.pop(0)
                    for e in range(ET):
                        last[e] = step(tap(e, k, CT, NT, k == VE_TAPS[0]))

            dve.wait_ge(pads_ready, 6)

            def norm4(j, n, bank):
                dve.wait_ge(*((t_woc, 1) if j == 4 else (t_wo, j + 1)))
                dve.wait_ge(rtok_ready, 1 if j == 4 else j + 2)
                v.tensor_tensor(h3[0:n, j, :], ps[0:n, bank, 0:D], r_tok[0:n, j, :], ADD).then_inc(h3_ready, 1)
                dve.wait_ge(h3_ready, 1 if j == 4 else j + 2)
                k = step(v.bn_stats(st4[0:n, j, :], h3[0:n, j, :]))
                dve.wait_ge(vec_step, k)
                k = step(v.bn_aggr(ag4[0:n, j, :], st4[0:n, j, :]))
                dve.wait_ge(vec_step, k)
                v.tensor_scalar(ve4[0:n, j:j + 1], ag4[0:n, j, 1:2], EPS5, None, ADD).then_inc(var4, 1)

            def apply4(j, n):
                dve.wait_ge(rs4_ready, 1 if j == 4 else j // 2 + 2)
                v.tensor_scalar(x4[0:n, j, :], h3[0:n, j, :], ag4[0:n, j, 0:1], rs4[0:n, j:j + 1], SUB, MUL
                                ).then_inc(x4_ready, 1)

            taps(VE_PARTS[0])
            step(v.tensor_reduce(cmask[:, :], ident[0:CT, 0:CT].rearrange("p (i b) -> p i b", b=NB), AX.X, ADD))
            norm4(4, CT, 5)
            taps(VE_PARTS[1])
            apply4(4, CT)
            taps(VE_PARTS[2])
            dve.wait_ge(t_g, 1)
            k = step(v.tensor_tensor(gsel[:, :, :], ps[0:CT, 5, 0:2 * NCLS].rearrange("p (i j) -> p i j", j=2),
                                     cmask[:, :].unsqueeze(2).broadcast_to([CT, NCLS, 2]), MUL))
            dve.wait_ge(vec_step, k)
            k = step(v.tensor_reduce(lg[:, :], gsel[:, :, :].rearrange("p i j -> p j i"), AX.X, ADD))
            dve.wait_ge(vec_step, k)
            k = step(v.tensor_reduce(g_mx[:, :], lg[:, :], AX.X, ALU.max))
            dve.wait_ge(vec_step, k)
            v.tensor_scalar(g_d[:, :], lg[:, :], g_mx[:, 0:1], None, SUB).then_inc(gmax_ready, 1)
            taps(VE_PARTS[3])
            dve.wait_ge(gexp_ready, 1)
            k = step(v.tensor_reduce(g_s[:, :], g_e[:, :], AX.X, ADD))
            dve.wait_ge(vec_step, k)
            k = step(v.reciprocal(g_s[:, :], g_s[:, :]))
            dve.wait_ge(vec_step, k)
            k = step(v.tensor_scalar(g_p[:, :], g_e[:, :], g_s[:, 0:1], None, MUL))
            dve.wait_ge(vec_step, k)
            k = step(v.tensor_reduce(g_mx[:, :], g_p[:, :], AX.X, ALU.min))
            dve.wait_ge(vec_step, k)
            k = step(v.tensor_scalar(g_m[:, :], g_p[:, :], g_mx[:, 0:1], None, ALU.is_gt))
            dve.wait_ge(vec_step, k)
            k = step(v.tensor_tensor(g_p[:, :], g_p[:, :], g_m[:, :], MUL))
            dve.wait_ge(vec_step, k)
            k = step(v.tensor_reduce(g_s[:, :], g_p[:, :], AX.X, ADD))
            dve.wait_ge(vec_step, k)
            k = step(v.tensor_scalar(g_s[:, :], g_s[:, :], EPS6, None, ALU.max))
            dve.wait_ge(vec_step, k)
            k = step(v.reciprocal(g_s[:, :], g_s[:, :]))
            dve.wait_ge(vec_step, k)
            k = step(v.tensor_scalar(gate[:, :], g_p[:, :], g_s[:, 0:1], None, MUL))
            dve.wait_ge(vec_step, k)
            taps(VE_PARTS[4])
            dve.wait_ge(t_dncls, 1)
            k = step(v.scalar_tensor_tensor(oc1[:, :], ps[0:CT, 0, 0:D], gate[:, 1:2], h3[0:CT, 4, :], MUL, ADD))
            dve.wait_ge(vec_step, k)
            dve.wait_ge(t_oc, 1)
            v.scalar_tensor_tensor(oc[:, :], ps[0:CT, 1, 0:D], gate[:, 0:1], oc1[:, :], MUL, ADD
                                   ).then_inc(oc_ready, 1)
            taps(len(todo))
            for c0, n in HALF:
                for e in range(ET):
                    dve.wait_ge(t_y, e + 1)
                    dve.wait_ge(vec_step, last[e])
                    dst = y[:, e, CT + c0:CT + c0 + n]
                    v.tensor_tensor(dst, ps[:, Y_BANK[e], c0:c0 + n], dst, ADD).then_inc(y_ready, 1)
            for q in range(2):
                for j in (2 * q, 2 * q + 1):
                    norm4(j, PTILES[j][1], WO_BANK[j])
                for j in (2 * q, 2 * q + 1):
                    apply4(j, PTILES[j][1])
            for j, (c0, n) in enumerate(PTILES):
                dve.wait_ge(t_dn, j + 1)
                dve.wait_ge(h3b_ready, j + 1)
                v.tensor_tensor(o[0:n, j, :], ps[0:n, WO_BANK[j], 0:D], h3b[0:n, j, :], ADD).then_inc(o_ready, 1)

        @block.tensor
        def _(pe):
            t = nc.tensor

            def mm(out_, lhsT, rhs, start, stop):
                return t.matmul(out_, lhsT, rhs, start=start, stop=stop, skip_group_check=True)

            def keep_warm(n, bank):
                for _ in range(n):
                    mm(ps[:, bank, 384:512], ident[:, :], ident[:, :], True, True)

            pe.wait_ge(ident_ready, 1)
            keep_warm(WARM, 7)

            def turn(i):
                pe.wait_ge(*((xr5_ready, 1) if i == KC - 1 else (xr_ready, i + 1)))
                if i >= 2:
                    pe.wait_ge(xT_ready, i - 1)
                for nw in range(NW):
                    ins = t.transpose(ps[:, 2 * (i % 2) + nw // 3, (nw % 3) * BH:(nw % 3 + 1) * BH],
                                      xr[:, i, nw, :], ident[0:BH, 0:BH])
                ins.then_inc(t_x, 1)

            def product(i, nws):
                c, hh = chunks[i]
                pe.wait_ge(Wp_ready, i + 1)
                pe.wait_ge(xT_ready, i + 1)
                for nw in nws:
                    mm(hbank(nw), xT[:, i, nw, :], Wp[:, hh, c, :], i == 0 and nw % 2 == 0, False)

            def fold(nws):
                for nw in nws:
                    mm(hbank(nw), ms1T[:, nw, :], fold_rows[:, :], False, True).then_inc(t_h, 1)

            turn(0)
            turn(1)
            pe.wait_ge(l_ln1, 32)
            pe.wait_ge(l_W, 16)
            for i, (c, hh) in enumerate(chunks):
                mm(ps[0:2, 7, 0:D], ln1_col[:, :, hh, c], W_sb[:, hh, c, :], i == 0, False)
            product(0, [0, 1])
            turn(2)
            product(0, [2, 3])
            product(1, [0, 1])
            pe.wait_ge(const_ready, 5)
            pe.wait_ge(l_tokb, 16)
            mm(ps[0:2, 7, 0:D], sel01[:, :], tokb_row[:, :], False, True).then_inc(t_rows, 1)
            turn(3)
            product(1, [2, 3])
            product(2, [0, 1])
            turn(4)
            product(2, [2, 3])
            product(3, [0, 1])
            turn(5)
            product(4, [0, 1])
            pe.wait_ge(rows_ready, 1)
            pe.wait_ge(nm1_ready, 1)
            pe.wait_ge(rs1_ready, 1)
            for nw in range(NW):
                out_ = ps[0:2, 7, D + nw * BH:D + (nw + 1) * BH] if nw < 3 else ps[0:2, 0, (nw - 3) * BH:(nw - 2) * BH]
                ins = t.transpose(out_, ms1[:, nw, :], ident[0:BH, 0:BH])
            ins.then_inc(t_ms1, 1)
            product(5, [0, 1])
            pe.wait_ge(ms1T_ready, 2)
            fold([0, 1])
            for i in range(3, KC):
                product(i, [2, 3])
            fold([2, 3])
            pe.wait_ge(l_Win, 32)
            for hh in range(2):
                for e in range(ET):
                    ins = t.transpose(ps[0:DH, hh, e * 128:(e + 1) * 128], Win_sb[:, e, hh * DH:(hh + 1) * DH],
                                      ident[:, :])
                ins.then_inc(t_w, 1)
            pe.wait_ge(l_Wout, 16)
            for e in range(ET):
                for hh in range(2):
                    c0 = (e % 2) * D + hh * DH
                    ins = t.transpose(ps[:, 2 + e // 2, c0:c0 + DH], Wout_sb[:, hh, e * 128:(e + 1) * 128],
                                      ident[0:DH, 0:DH])
                if e >= 1:
                    ins.then_inc(t_w, 1)
            pe.wait_ge(xs_ready, 1)
            for hh in range(2):
                ins = t.transpose(ps[0:DH, 7, hh * NB:(hh + 1) * NB], xs[0:NB, NW, hh * DH:(hh + 1) * DH],
                                  ident[0:NB, 0:NB])
            ins.then_inc(t_xs, 1)
            for i in range(KC):
                product(i, [4, 5])
            fold([4, 5])

            pe.wait_ge(wT_ready, 4)
            pe.wait_ge(pads_ready, 6)
            for q in range(NPAIR):
                pe.wait_ge(xs_ready, 2 * q + 3)
                for nw in pair(q):
                    for hh in range(2):
                        c0 = (2 * (nw % 2) + hh) * BH
                        ins = t.transpose(ps[0:DH, q % 2, c0:c0 + BH], xs[:, nw, hh * DH:(hh + 1) * DH],
                                          ident[0:BH, 0:BH])
                ins.then_inc(t_xs, 1)
                pe.wait_ge(xnT_ready, q + 2)
                c0, c1 = xn_cols(q)
                for e in range(ET):
                    i = q * ET + e
                    if i >= 5:
                        pe.wait_ge(xp_ready, {5: 3, 7: 6, 8: 9}.get(i, 3))
                    for hh in range(2):
                        ins = mm(ps[:, XP_BANK[i], 0:c1 - c0], WinT[0:KH[hh], hh, e * 128:(e + 1) * 128],
                                 xnT[0:KH[hh], hh, c0:c1], hh == 0, hh == 1)
                    ins.then_inc(t_xp, 1)

            todo = list(range(NDG))

            def taps(n):
                for _ in range(min(n, len(todo))):
                    i = todo.pop(0)
                    k = PE_TAPS[i]
                    lo = max(CT, k * NB)
                    for e in range(ET):
                        if i == 0:
                            pe.wait_ge(xp_ready, XP_DONE[e])
                        pe.wait_ge(diag_ready, i * ET + e + 1)
                        ins = mm(ps[:, Y_BANK[e], lo - CT:PT], diag[:, i, e, :], xp[:, e, lo - k * NB:NT - k * NB],
                                 i == 0, i == NDG - 1)
                        if i == NDG - 1:
                            ins.then_inc(t_y, 1)

            def project(cols, n, bank, done):
                for e in range(ET):
                    ins = mm(ps[0:n, bank, 0:D], y[:, e, cols:cols + n], WoutT[:, e, :], e == 0, e == ET - 1)
                ins.then_inc(done, 1)

            taps(PE_PARTS[0])
            pe.wait_ge(ycls_ready, ET)
            pe.wait_ge(wT_ready, 4)
            project(0, CT, 5, t_woc)
            taps(PE_PARTS[1])
            pe.wait_ge(x4_ready, 1)
            for hh in range(2):
                ins = t.transpose(ps[0:DH, 6, hh * CT:(hh + 1) * CT], x4[0:CT, 4, hh * DH:(hh + 1) * DH],
                                  ident[0:CT, 0:CT])
            ins.then_inc(t_x4c, 1)
            taps(PE_PARTS[2])
            pe.wait_ge(x4T_ready, 3)
            pe.wait_ge(l_G, 32)
            for hh in range(2):
                ins = mm(ps[0:CT, 5, 0:2 * NCLS], x4T[0:DH, hh, 0:CT], G_sb[:, hh].rearrange("p i j -> p (i j)"),
                         hh == 0, hh == 1)
            ins.then_inc(t_g, 1)
            pe.wait_ge(l_A1, 16 * (NEXP + 1))
            for k in range(2):
                for hh in range(2):
                    for a in range(NLO):
                        ins = mm(ps[32 * a:32 * a + 32, k, 0:HH], x4T[0:KH[hh], hh, 32 * a:32 * a + 32],
                                 A1_sb[0:KH[hh], a, hh, k * HH:(k + 1) * HH], hh == 0, hh == 1)
            ins.then_inc(t_uplo, 1)
            for k in range(2):
                for hh in range(2):
                    for a in range(NHI):
                        ins = mm(ps[64 * a:64 * a + 64, 6 + k, 0:HH], x_par[0:KH[hh], hh, a, :],
                                 A1_sb[0:KH[hh], NLO + a, hh, k * HH:(k + 1) * HH], hh == 0, hh == 1)
            ins.then_inc(t_uphi, 1)
            taps(PE_PARTS[3])
            pe.wait_ge(hlo_ready, 1)
            for m in range(M):
                ins = t.transpose(ps[:, m // M2, (m % M2) * CT:(m % M2 + 1) * CT], hid_lo[:, m * 128:(m + 1) * 128],
                                  ident[0:CT, 0:CT])
                if m % M2 == M2 - 1:
                    ins.then_inc(t_tlo, 1)
            taps(PE_PARTS[4])
            pe.wait_ge(hhi_ready, 1)
            for m in range(M):
                ins = t.transpose(ps[:, 6 + m // M2, (m % M2) * 128:(m % M2 + 1) * 128],
                                  hid_hi[:, m * 128:(m + 1) * 128], ident[:, :])
                if m % M2 == M2 - 1:
                    ins.then_inc(t_thi, 1)
            taps(PE_PARTS[5])
            pe.wait_ge(l_A2, 16 * NEXP)
            pe.wait_ge(l_A2b, 16)
            pe.wait_ge(gmax_ready, 1)
            pe.wait_ge(hpar_ready, 4)
            for m in range(M):
                for j in range(NHI):
                    mm(ps[64 * j:64 * j + 64, 5, 0:D], hid_par[:, m, j, :], A2_sb[:, NLO + j, m, :], m == 0, False)
            for j in range(NHI):
                ins = mm(ps[64 * j:64 * j + 64, 5, 0:D], ones[:, 0:64], A2b_row[:, NLO + j, :], False, True)
            ins.then_inc(t_dnpar, 1)
            pe.wait_ge(hcls_ready, 4)
            for m in range(M):
                for c in range(NLO):
                    mm(ps[32 * c:32 * c + 32, 0, 0:D], hid_cls[:, m, 32 * c:32 * c + 32], A2_sb[:, c, m, :],
                       m == 0, False)
            for c in range(NLO):
                ins = mm(ps[32 * c:32 * c + 32, 0, 0:D], ones[:, 0:32], A2b_row[:, c, :], False, True)
            ins.then_inc(t_dncls, 1)
            taps(PE_PARTS[6])
            pe.wait_ge(opar_ready, 1)
            pe.wait_ge(perm_ready, 2)
            mm(ps[0:CT, 1, 0:D], perm[:, :, :, :].rearrange("p i j b -> p (i j b)"), o_par[:, :], True, True
               ).then_inc(t_oc, 1)
            taps(len(todo))

            for j, (c0, n) in enumerate(PTILES):
                pe.wait_ge(y_ready, ET * (1 + j // 2))
                if j == 1:
                    pe.wait_ge(oc_ready, 1)
                project(CT + c0, n, WO_BANK[j], t_wo)
            pe.wait_ge(l_W1, 32)
            for q, (h0, hn) in enumerate(HALF):
                for j in (2 * q, 2 * q + 1):
                    n = PTILES[j][1]
                    pe.wait_ge(x4_ready, j + 2)
                    if q == 1:
                        pe.wait_ge(hid_ready, j + 1)
                    for hh in range(2):
                        ins = t.transpose(ps[0:DH, X4_BANK[j], hh * n:(hh + 1) * n],
                                          x4[0:n, j, hh * DH:(hh + 1) * DH], ident[0:n, 0:n])
                    ins.then_inc(t_x4, 1)
                pe.wait_ge(x4T_ready, 3 + 2 * (q + 1))
                for m in range(M):
                    i = q * M + m
                    if i >= 4:
                        pe.wait_ge(hid_ready, i - 3)
                    for hh in range(2):
                        ins = mm(ps[:, UP_BANK[i % 4], 0:hn], W1_sb[0:KH[hh], hh, m * 128:(m + 1) * 128],
                                 x4T[0:KH[hh], hh, CT + h0:CT + h0 + hn], hh == 0, hh == 1)
                    ins.then_inc(t_up, 1)
            pe.wait_ge(l_W2, 16)
            for j, (c0, n) in enumerate(PTILES):
                for m in range(M):
                    pe.wait_ge(hid_ready, (j // 2) * M + m + 1)
                    ins = mm(ps[0:n, WO_BANK[j], 0:D], hid[:, m, c0:c0 + n], W2_sb[:, m, :], m == 0, m == M - 1)
                ins.then_inc(t_dn, 1)


_INS = ['x', 'L0_tok_ln1_w', 'L0_tok_ln1_b', 'L0_tok_W', 'L0_tok_b', 'L0_tok_ln2_w', 'L0_tok_ln2_b',
        'L0_tok_cls', 'L0_tok_pos', 'L0_attn_gamma', 'L0_attn_W_in', 'L0_attn_b_in', 'L0_attn_conv_w',
        'L0_attn_A', 'L0_attn_Bp', 'L0_attn_C', 'L0_attn_W_out', 'L0_attn_b_out', 'L0_ffn_moe0_W1',
        'L0_ffn_moe0_b1', 'L0_ffn_moe0_W2', 'L0_ffn_moe0_b2', 'L0_ffn_A1_W', 'L0_ffn_A1_b', 'L0_ffn_A2_W',
        'L0_ffn_A2_b', 'L0_ffn_G_W']


def kernel(**inputs):
    import numpy as _np
    import concourse.bacc as _bacc
    from concourse import mybir as _mybir
    from concourse.bass_utils import run_bass_kernel_spmd as _run

    nc = _bacc.Bacc("TRN2", target_bir_lowering=False, num_devices=1)
    arrays, args = {}, []
    for name in _INS:
        a = _np.ascontiguousarray(inputs[name])
        arrays[f"in_{name}_dram"] = a
        args.append(nc.dram_tensor(f"in_{name}_dram", a.shape, _mybir.dt.from_np(a.dtype), kind="ExternalInput").ap())
    shape = (inputs['x'].shape[0], 37, 192)
    args.append(nc.dram_tensor("out_0_dram", shape, _mybir.dt.float32, kind="ExternalOutput").ap())
    vit_tower_kernel(nc, *args)
    res = _run(nc, [arrays], core_ids=[0])
    return res.results[0]["out_0_dram"]
```

```python
import concourse.bass as bass
from concourse import mybir
from contextlib import ExitStack


def vit_tower_kernel(nc, x, ln1_w, ln1_b, tok_W, tok_b, ln2_w, ln2_b, cls, pos,
                     gamma, W_in, b_in, conv_w, A, Bp, C, W_out, b_out,
                     m0_W1, m0_b1, m0_W2, m0_b2, A1_W, A1_b, A2_W, A2_b, G_W, out):
    F32 = mybir.dt.float32
    ALU = mybir.AluOpType
    ACT = mybir.ActivationFunctionType
    AX = mybir.AxisListType
    MUL, ADD, SUB = ALU.mult, ALU.add, ALU.subtract

    NB, NC, IMG, _ = x.shape
    P = 16
    NH = NW = IMG // P
    BH = NB * NH
    D = tok_W.shape[1]
    DH = D // 2
    T = NH * NW + 1
    NT = NB * T
    E = W_in.shape[0]
    ET = E // 128
    NST = A.shape[1]
    DC = conv_w.shape[1]
    NCLS = 6
    CT = NCLS * NB
    PT = NT - CT
    HID = m0_W1.shape[1]
    M = HID // 128
    NEXP = A1_W.shape[0]
    HB = 8
    H2 = P // HB
    KC = NC * H2
    EPS5, EPS6 = 1e-5, 1e-6
    PTILES = [(0, 128), (128, 128), (256, 128), (384, PT - 384)]
    HALF = [(0, 256), (256, PT - 256)]
    NLO, NHI = 3, 2
    PE_TAPS = [[0, 1, 2, 3, 4, 7, 8, 9], [0, 1, 2, 3]]
    PE_PARTS = [4, 3, 1, 1, 1]
    GP_TAPS = [[5] + list(range(14, 22)), [5] + list(range(23, T))]
    GP_PARTS = [3, 4]
    AC_PARTS = [8, 3, 2, 4, 1, 2]
    VE_BOTH = [6, 10, 11]
    VE_TAPS = [[k for k in range(h0 // NB + n // NB + NCLS) if k not in PE_TAPS[q] + GP_TAPS[q] + VE_BOTH]
               for q, (h0, n) in enumerate(HALF)]
    VE_PARTS = [2, 1, 4, 1, 1, 3, 2]
    DIAGS = sorted(set(PE_TAPS[0] + PE_TAPS[1]))
    for q in range(2):
        for k in (PE_TAPS[q][0], GP_TAPS[q][0], VE_BOTH[0]):
            assert k * NB <= CT + HALF[q][0]
    NDG = len(DIAGS)
    VE_LEFT0 = len(VE_BOTH) + len(VE_TAPS[0]) - VE_PARTS[0] - VE_PARTS[1]
    NTMP = 3
    WARM = 9
    GAP_WARM = 4

    ctx = ExitStack()
    with ctx:
        def sb(name, shape):
            return ctx.enter_context(nc.sbuf_tensor(name, shape, F32))

        def within(area, offset, shape):
            n = 1
            for d in shape[1:]:
                n *= d
            v = area[0:shape[0], offset:offset + n]
            if len(shape) > 2:
                names = "abcd"[:len(shape) - 1]
                v = v.rearrange(f"p ({' '.join(names)}) -> p {' '.join(names)}",
                                **{k: d for k, d in zip(names[1:], shape[2:])})
            return v

        def sem(name):
            return ctx.enter_context(nc.semaphore(name))

        ident = sb("ident", [128, 128])
        ones = sb("ones", [1, 64])
        sel01 = sb("sel01", [1, 2])
        table_row = sb("table_row", [1, 1])
        half = sb("half", [BH, NW])
        eps5 = sb("eps5", [128, 1])
        neg_half = sb("neg_half", [128, 2])
        pixel_area = sb("pixel_area", [128, NC * P * IMG])
        x_sb = within(pixel_area, 0, [BH, NC, P * IMG])
        hid = within(pixel_area, 0, [128, M, PT])
        hid_lo = within(pixel_area, M * PT, [CT, HID])
        hid_hi = within(pixel_area, M * PT + HID, [128, HID])
        line_area = sb("line_area", [128, NEXP * M * D])
        xr = within(line_area, 0, [BH, KC, NW, 128])
        A2_sb = within(line_area, 0, [128, NEXP, M, D])
        xT_area = sb("xT_area", [128, KC * NW * BH])
        xT = within(xT_area, 0, [128, KC, NW, BH])
        h3 = within(xT_area, 0, [128, 5, D])
        h3b = within(xT_area, 5 * D, [128, 5, D])
        x4 = within(xT_area, 10 * D, [128, 5, D])
        hid_cls = within(xT_area, 15 * D, [128, M, CT])
        powr_area = sb("powr_area", [128, T * ET * NST])
        powr = within(powr_area, 0, [128, T, ET * NST])
        ptmp = sb("ptmp", [128, NTMP, ET, HALF[0][1]])
        yg = within(powr_area, 0, [128, ET, PT])
        diag = sb("diag", [128, NDG, ET, 128])
        xp = sb("xp", [128, ET, NT])
        tok_area = sb("tok_area", [128, ET * NT])
        h = within(tok_area, 0, [BH, NW, D])
        y = within(tok_area, 0, [128, ET, NT])
        Wp_area = sb("Wp_area", [128, KC * D])
        Wp = within(Wp_area, 0, [128, H2, NC, D])
        o = within(Wp_area, 0, [128, 4, D])
        W_area = sb("W_area", [128, KC * D])
        W_sb = within(W_area, 0, [128, H2, NC, D])
        W2_sb = within(W_area, 0, [128, M, D])
        ln1_col = sb("ln1_col", [128, 2, H2, NC])
        tokb_row = sb("tokb_row", [1, D])
        fold_rows = sb("fold_rows", [2, D])
        gamma_col = sb("gamma_col", [DH, 2])
        A2b_row = sb("A2b_row", [1, NEXP, D])
        ssm = sb("ssm", [128, 3, ET, NST])
        cw = sb("cw", [128, ET, DC])
        sq = sb("sq", [128, 6, ET * NST])
        Gk = sb("Gk", [128, T, ET])
        Kk = sb("Kk", [128, T, ET])
        ktmp = within(tok_area, NW * D, [128, DC, T, ET])
        ln2w_bc = sb("ln2w_bc", [BH, D])
        ln2b_bc = sb("ln2b_bc", [BH, D])
        posb = sb("posb", [BH, NW, D])
        bout_bc = sb("bout_bc", [128, D])
        m0b2_bc = sb("m0b2_bc", [128, D])
        cls_sb = sb("cls_sb", [NB, D])
        pos0_sb = sb("pos0_sb", [NB, D])
        st1 = sb("st1", [BH, NW, NC, 6])
        ag1 = sb("ag1", [BH, NW, 2])
        ve1 = sb("ve1", [BH, NW])
        ms1 = sb("ms1", [BH, NW, 2])
        ms1T = sb("ms1T", [2, NW, BH])
        st2 = sb("st2", [BH, NW, 6])
        ag2 = sb("ag2", [BH, NW, 2])
        ve2 = sb("ve2", [BH, NW])
        rs2 = sb("rs2", [BH, NW])
        h2 = sb("h2", [BH, NW + 1, D])
        st3 = sb("st3", [BH, NW + 1, 6])
        ag3 = sb("ag3", [BH, NW + 1, 2])
        s3 = sb("s3", [BH, 2, NW + 1])
        one3 = sb("one3", [BH, NW + 1])
        nm3 = sb("nm3", [BH, NW + 1])
        nb3 = sb("nb3", [BH, NW])
        xs = sb("xs", [BH, NW + 1, D])
        r = sb("r", [BH, NW + 1, D])
        Win_sb = sb("Win_sb", [128, ET, D])
        Wout_sb = sb("Wout_sb", [DH, 2, E])
        WinT = sb("WinT", [DH + 1, 2, E])
        WoutT = sb("WoutT", [128, ET, D])
        xnT = sb("xnT", [DH + 1, 2, NT])
        r_tok = sb("r_tok", [128, 5, D])
        st4 = sb("st4", [128, 5, 6])
        ag4 = sb("ag4", [128, 5, 2])
        ve4 = sb("ve4", [128, 5])
        rs4 = sb("rs4", [128, 5])
        x4T = sb("x4T", [DH + 1, 2, NT])
        x_par = sb("x_par", [DH + 1, 2, 2, 64])
        perm = sb("perm", [128, NCLS // 2, 2, NB])
        hid_par = sb("hid_par", [128, M, 2, 64])
        o_par = sb("o_par", [128, D])
        A1_sb = sb("A1_sb", [DH + 1, NEXP, 2, HID])
        W1_sb = sb("W1_sb", [DH + 1, 2, HID])
        G_sb = sb("G_sb", [DH, 2, NCLS, 2])
        cmask = sb("cmask", [CT, NCLS])
        gsel = sb("gsel", [CT, NCLS, 2])
        lg = sb("lg", [CT, 2])
        g_mx = sb("g_mx", [CT, 1])
        g_d = sb("g_d", [CT, 2])
        g_e = sb("g_e", [CT, 2])
        g_s = sb("g_s", [CT, 1])
        g_p = sb("g_p", [CT, 2])
        g_m = sb("g_m", [CT, 2])
        gate = sb("gate", [CT, 2])
        oc1, oc = xs[0:CT, 0, :], xs[0:CT, 1, :]
        ps = ctx.enter_context(nc.psum_tensor("ps", [128, 8, 512], F32))
        r_dram = nc.dram_tensor("r_scratch", [NT, D], F32).ap()

        l_ln1, l_ssm, l_cw, l_W, l_tokb, l_cls, l_ln2, l_pos = [sem(f"l_{n}") for n in (
            "ln1", "ssm", "cw", "W", "tokb", "cls", "ln2", "pos")]
        l_x = [sem(f"l_x{c}") for c in range(NC)]
        l_bc, l_Win, l_Wout, l_gamma, l_G, l_A1, l_A2, l_A2b, l_W1, l_W2 = [sem(f"l_{n}") for n in (
            "bc", "Win", "Wout", "gamma", "G", "A1", "A2", "A2b", "W1", "W2")]
        s_rw = sem("s_rw")
        l_rc = sem("l_rc")
        l_rp = sem("l_rp")
        s_out = sem("s_out")
        pool_step = sem("pool_step")
        ident_ready = sem("ident_ready")
        const_ready = sem("const_ready")
        posb_ready = sem("posb_ready")
        perm_ready = sem("perm_ready")
        diag_ready = sem("diag_ready")
        co_ready = sem("co_ready")
        xr5_ready = sem("xr5_ready")
        rs1_ready = sem("rs1_ready")
        K_ready = sem("K_ready")
        rtok_ready = sem("rtok_ready")
        rs4_ready = sem("rs4_ready")
        h3b_ready = sem("h3b_ready")
        prod_used = sem("prod_used")
        vec_step = sem("vec_step")
        pads_ready = sem("pads_ready")
        Wp_ready = sem("Wp_ready")
        nm1_ready = sem("nm1_ready")
        var1, var2, var3, var4 = [sem(f"var{i}") for i in range(1, 5)]
        h_read = sem("h_read")
        rc_ready = sem("rc_ready")
        r_ready = sem("r_ready")
        rv_ready = sem("rv_ready")
        xs_ready = sem("xs_ready")
        nb_ready = sem("nb_ready")
        ycls_ready = sem("ycls_ready")
        y_ready = sem("y_ready")
        h3_ready = sem("h3_ready")
        x4_ready = sem("x4_ready")
        gmax_ready = sem("gmax_ready")
        oc_ready = sem("oc_ready")
        o_ready = sem("o_ready")
        prod_ready = sem("prod_ready")
        sig_ready, rows_ready, ms1T_ready, xr_ready, xT_ready, wT_ready = [sem(n) for n in (
            "sig_ready", "rows_ready", "ms1T_ready", "xr_ready", "xT_ready", "wT_ready")]
        rs2_ready, rs3_ready = [sem(f"rs{i}_ready") for i in (2, 3)]
        xa_ready = sem("xa_ready")
        xnT_ready, xp_ready, x4T_ready, gexp_ready = [sem(n) for n in (
            "xnT_ready", "xp_ready", "x4T_ready", "gexp_ready")]
        hlo_ready, hhi_ready, hpar_ready, hcls_ready, opar_ready, hid_ready = [sem(n) for n in (
            "hlo_ready", "hhi_ready", "hpar_ready", "hcls_ready", "opar_ready", "hid_ready")]
        t_rows, t_ms1, t_x, t_h, t_w, t_xs, t_xp, t_y, t_woc, t_wo, t_x4c, t_x4, t_g = [sem(f"t_{n}") for n in (
            "rows", "ms1", "x", "h", "w", "xs", "xp", "y", "woc", "wo", "x4c", "x4", "g")]
        t_uplo, t_uphi, t_tlo, t_thi, t_dnpar, t_dncls, t_oc, t_up, t_dn = [sem(f"t_{n}") for n in (
            "uplo", "uphi", "tlo", "thi", "dnpar", "dncls", "oc", "up", "dn")]

        chunks = [(c, hh) for c in range(NC) for hh in range(H2)]
        x_pix = x_sb.rearrange("p c (y n w) -> p c y n w", y=P, n=NW)
        WO_SLOT = [(5, 0), (5, D), (2, 0), (3, 0)]
        DN_BANK = [0, 5, 2, 3]
        X4_BANK = [1, 4]
        UP_BANK = [6, 7, 1]
        Y_BANK = [2, 3, 4]
        XP_BANK = [2, 3, 7, 4, 5, 2, 6, 3, 7]
        XP_DONE = [NW * ET + ET - 2 * (ET - 1 - e) for e in range(ET)]
        NPAIR = NW // 2
        KH = [DH + 1, DH]
        HH = HID // 2
        M2 = M // 2

        def hbank(nw):
            return ps[0:BH, 4 + nw // 2, (nw % 2) * D:(nw % 2 + 1) * D]

        def pair(q):
            return [2 * q, 2 * q + 1]

        def xn_cols(q):
            return (0 if q == 0 else NB + 2 * q * BH), NB + 2 * (q + 1) * BH

        block = ctx.enter_context(nc.Block())

        @block.sync
        def _(sp):
            def load_x(c):
                sp.dma_start(x_sb[:, c, :], x[:, c].rearrange("b (n q) w -> b n (q w)", n=NH)).then_inc(l_x[c], 16)

            load_x(0)
            sp.dma_start(W_sb.rearrange("p h c d -> p h (c d)"),
                         tok_W.rearrange("(h p c) d -> p h (c d)", h=H2, c=NC)).then_inc(l_W, 16)
            sp.dma_start(ln1_col[:, 0], ln1_w.rearrange("(h p c) -> p h c", h=H2, c=NC)).then_inc(l_ln1, 16)
            sp.dma_start(ln1_col[:, 1], ln1_b.rearrange("(h p c) -> p h c", h=H2, c=NC)).then_inc(l_ln1, 16)
            load_x(1)
            load_x(2)
            sp.dma_start(ln2w_bc[:, :], ln2_w.partition_broadcast(BH)).then_inc(l_ln2, 16)
            sp.dma_start(ln2b_bc[:, :], ln2_b.partition_broadcast(BH)).then_inc(l_ln2, 16)
            sp.dma_start(posb[:, :, :].rearrange("p n d -> p (n d)"),
                         pos[1:T].rearrange("(n w) d -> n (w d)", w=NW).unsqueeze(0).broadcast_to(
                             [NB, NH, NW * D])).then_inc(l_pos, 16)
            for hh in range(2):
                sp.dma_start(gamma_col[:, hh:hh + 1], gamma[hh * DH:(hh + 1) * DH].unsqueeze(1)).then_inc(l_gamma, 16)
            sp.dma_start(Win_sb[:, :, :], W_in.rearrange("(e p) d -> p e d", p=128)).then_inc(l_Win, 16)
            sp.dma_start(WinT[DH:DH + 1, 0, :], b_in.unsqueeze(0)).then_inc(l_Win, 16)
            sp.dma_start(Wout_sb[:, :, :], W_out.rearrange("(h p) e -> p h e", p=DH)).then_inc(l_Wout, 16)
            for hh in range(2):
                sp.dma_start(G_sb[:, hh], G_W[:, hh * DH:(hh + 1) * DH, :].rearrange("i p j -> p i j")
                             ).then_inc(l_G, 16)
            for a in range(NEXP):
                sp.dma_start(A1_sb[0:DH, a], A1_W[a].rearrange("(h p) f -> p h f", p=DH)).then_inc(l_A1, 16)
            sp.dma_start(A1_sb[DH:DH + 1, :, 0, :], A1_b.unsqueeze(0)).then_inc(l_A1, 16)
            sp.dma_start(A2b_row[:, :, :], A2_b.unsqueeze(0)).then_inc(l_A2b, 16)
            sp.dma_start(bout_bc[:, :], b_out.partition_broadcast(128)).then_inc(l_bc, 16)
            sp.dma_start(m0b2_bc[:, :], m0_b2.partition_broadcast(128)).then_inc(l_bc, 16)
            sp.dma_start(W1_sb[0:DH, :, :], m0_W1.rearrange("(h p) f -> p h f", p=DH)).then_inc(l_W1, 16)
            sp.dma_start(W1_sb[DH:DH + 1, 0, :], m0_b1.unsqueeze(0)).then_inc(l_W1, 16)
            sp.wait_ge(t_x, KC)
            sp.wait_ge(Wp_ready, KC)
            sp.dma_start(W2_sb[:, :, :], m0_W2.rearrange("(m p) d -> p m d", p=128)).then_inc(l_W2, 16)
            for a in range(NEXP):
                sp.dma_start(A2_sb[:, a], A2_W[a].rearrange("(m p) d -> p m d", p=128)).then_inc(l_A2, 16)
            r_rows = r_dram.rearrange("(t b) d -> t b d", b=NB)
            sp.wait_ge(r_ready, 1)
            sp.dma_start(r_rows[0], r[0:NB, NW, :]).then_inc(s_rw, 16)
            for nw in range(NW):
                sp.wait_ge(*((r_ready, nw + 2) if nw < 2 else (rv_ready, nw - 1)))
                sp.dma_start(r_rows[1 + nw:T:NW].rearrange("n b d -> b n d"), r[:, nw, :]).then_inc(s_rw, 16)
            sp.wait_ge(s_rw, 16 * (NW + 1))
            sp.dma_start(r_tok[0:CT, 4, :], r_dram[0:CT]).then_inc(l_rc, 16)
            sp.dma_start(r_tok[:, 0:3, :], r_dram[CT:CT + 384].rearrange("(j p) d -> p j d", p=128)
                         ).then_inc(l_rp, 16)
            sp.dma_start(r_tok[0:PTILES[3][1], 3, :], r_dram[CT + 384:NT]).then_inc(l_rp, 16)
            o_rows = out.rearrange("b t d -> t b d")
            sp.wait_ge(oc_ready, 1)
            sp.dma_start(o_rows[0:NCLS], oc).then_inc(s_out, 16)
            for j, (c0, n) in enumerate(PTILES):
                t0 = NCLS + c0 // NB
                sp.wait_ge(o_ready, j + 1)
                sp.dma_start(o_rows[t0:t0 + n // NB], o[0:n, j, :]).then_inc(s_out, 16)
            sp.wait_ge(s_out, 16 * 5)

        @block.gpsimd
        def _(pool):
            g = nc.gpsimd
            n_step = [0]

            def step(ins):
                n_step[0] += 1
                ins.then_inc(pool_step, 1)
                return n_step[0]

            k = step(g.memset(ident[:, :], 0.0))
            pool.wait_ge(pool_step, k)
            g.affine_select(out=ident[:, :], in_=ident[:, :], compare_op=ALU.not_equal, fill=1.0,
                            base=0, pattern=[[-1, 128]], channel_multiplier=1).then_inc(ident_ready, 1)
            g.memset(ones[:, :], 1.0).then_inc(const_ready, 1)
            g.memset(sel01[:, 0:1], 0.0).then_inc(const_ready, 1)
            g.memset(sel01[:, 1:2], 1.0).then_inc(const_ready, 1)
            g.memset(neg_half[:, :], -0.5).then_inc(const_ready, 1)
            g.memset(eps5[:, :], EPS5).then_inc(const_ready, 1)
            g.memset(half[:, :], 0.5).then_inc(const_ready, 1)
            for i, v in enumerate((A, Bp, C)):
                pool.dma_start(ssm[:, i], v.rearrange("(e p) n -> p e n", p=128)).then_inc(l_ssm, 16)
            pool.dma_start(tokb_row[:, :], tok_b.unsqueeze(0)).then_inc(l_tokb, 16)
            pool.dma_start(cls_sb[:, :], cls[0].partition_broadcast(NB)).then_inc(l_cls, 16)
            pool.dma_start(pos0_sb[:, :], pos[0].partition_broadcast(NB)).then_inc(l_cls, 16)
            pool.dma_start(cw[:, :, :], conv_w.rearrange("(e p) n -> p e n", p=128)).then_inc(l_cw, 16)
            pool.wait_ge(ident_ready, 1)
            c, hh = chunks[KC - 1]
            pool.wait_ge(l_x[c], 16)
            g.tensor_scalar(xr[:, KC - 1].rearrange("p n (y w) -> p n y w", y=HB),
                            x_pix[:, c, hh * HB:(hh + 1) * HB].rearrange("p y n w -> p n y w"),
                            1.0, 1.0, MUL, MUL).then_inc(xr5_ready, 1)
            pool.wait_ge(const_ready, 6)
            pool.wait_ge(nm1_ready, 2)
            g.tensor_tensor(ms1[:, :, 1], ms1[:, :, 1], half[:, :], ALU.pow).then_inc(rs1_ready, 1)
            pool.wait_ge(l_pos, 16)
            pool.wait_ge(l_ln2, 32)
            g.tensor_tensor(posb[:, :, :], posb[:, :, :], ln2b_bc[:, :].unsqueeze(1).broadcast_to([BH, NW, D]),
                            ADD).then_inc(posb_ready, 1)
            def residual_scales(n, s, count):
                pool.wait_ge(rc_ready, count)
                k = step(g.tensor_scalar(nm3[0:n, s], ag3[0:n, s, 0], -1.0, 1.0, MUL, MUL))
                g.tensor_scalar(one3[0:n, s], s3[0:n, 0, s], 1.0, 1.0, MUL, ADD).then_inc(co_ready, 1)
                pool.wait_ge(pool_step, k)
                g.tensor_tensor(nm3[0:n, s], nm3[0:n, s], s3[0:n, 0, s], MUL).then_inc(co_ready, 1)

            pool.wait_ge(sig_ready, 1)
            sA = ssm[:, 0].rearrange("p e n -> p (e n)")
            k = step(g.tensor_tensor(powr[:, 0, :], ssm[:, 1].rearrange("p e n -> p (e n)"),
                                     ssm[:, 2].rearrange("p e n -> p (e n)"), MUL))
            pool.wait_ge(pool_step, k)
            k = step(g.tensor_tensor(powr[:, 1, :], powr[:, 0, :], sA, MUL))
            base, cur, i = sA, 2, 0
            while cur < T:
                k = step(g.tensor_tensor(sq[:, i, :], base, base, MUL))
                pool.wait_ge(pool_step, k)
                base = sq[:, i, :]
                n = min(cur, T - cur)
                ins = g.tensor_tensor(powr[:, cur:cur + n, :], powr[:, 0:n, :],
                                      base.unsqueeze(1).broadcast_to([128, n, ET * NST]), MUL)
                cur, i = cur + n, i + 1
                k = step(ins)
            residual_scales(NB, slice(NW, NW + 1), 1)
            pw4 = powr.rearrange("p k (e n) -> p k e n", e=ET)
            n = NST
            while n > 1:
                n //= 2
                pool.wait_ge(pool_step, k)
                dst = Gk[:, :, :].unsqueeze(3) if n == 1 else pw4[:, :, :, 0:n]
                k = step(g.tensor_tensor(dst, pw4[:, :, :, 0:n], pw4[:, :, :, n:2 * n], ADD))
            residual_scales(BH, slice(0, 2), 2)
            pool.wait_ge(l_cw, 16)
            pool.wait_ge(pool_step, k)
            for j in range(DC):
                dst = Kk[:, :, :] if j == 0 else ktmp[:, j, j:T, :]
                k = step(g.tensor_tensor(dst, Gk[:, 0:T - j, :],
                                         cw[:, :, DC - 1 - j].unsqueeze(1).broadcast_to([128, T - j, ET]), MUL))
            for j in range(1, DC):
                pool.wait_ge(pool_step, k)
                ins = g.tensor_tensor(Kk[:, j:T, :], Kk[:, j:T, :], ktmp[:, j, j:T, :], ADD)
                if j < DC - 1:
                    k = step(ins)
                else:
                    ins.then_inc(K_ready, 1)
            for j in range(2):
                g.tensor_scalar(perm[:, :, j, :],
                                ident[:, 64 * j:64 * j + CT // 2].rearrange("p (i b) -> p i b", b=NB),
                                1.0, 1.0, MUL, MUL).then_inc(perm_ready, 1)
            pool.wait_ge(K_ready, 1)
            for i, k in enumerate(DIAGS):
                for e in range(ET):
                    g.tensor_scalar(diag[:, i, e, :], ident[:, :], Kk[:, k, e:e + 1], 1.0, MUL, MUL
                                    ).then_inc(diag_ready, 1)

            todo = [(q, k) for q in range(2) for k in GP_TAPS[q]]
            n_prod = [0, 0]

            def taps(n):
                for _ in range(min(n, len(todo))):
                    q, k = todo.pop(0)
                    c0, n_ = HALF[q]
                    lo = max(CT + c0, k * NB) - CT
                    n_prod[1] += 1
                    pool.wait_ge(prod_ready, ET * n_prod[1])
                    if k == GP_TAPS[q][0]:
                        continue
                    if n_prod[0] > 0:
                        pool.wait_ge(prod_used, n_prod[0])
                    b = n_prod[0] % NTMP
                    n_prod[0] += 1
                    dst = yg[:, :, lo:c0 + n_]
                    g.tensor_tensor(dst, dst, ptmp[:, b, :, lo - c0:n_], ADD).then_inc(prod_used, 1)

            taps(GP_PARTS[0])
            pool.wait_ge(l_bc, 32)
            pool.wait_ge(l_rc, 16)
            g.tensor_tensor(r_tok[0:CT, 4, :], r_tok[0:CT, 4, :], bout_bc[0:CT, :], ADD).then_inc(rtok_ready, 1)
            pool.wait_ge(var4, 1)
            g.tensor_tensor(rs4[0:CT, 4:5], ve4[0:CT, 4:5], neg_half[0:CT, 0:1], ALU.pow).then_inc(rs4_ready, 1)
            taps(len([1 for q, k in todo if q == 0]))
            pool.wait_ge(l_rp, 32)
            for j, (c0, n) in enumerate(PTILES):
                g.tensor_tensor(r_tok[0:n, j, :], r_tok[0:n, j, :], bout_bc[0:n, :], ADD).then_inc(rtok_ready, 1)

            def roots4(q):
                pool.wait_ge(pads_ready, 6)
                pool.wait_ge(var4, 2 * q + 3)
                g.tensor_tensor(rs4[0:128, 2 * q:2 * q + 2], ve4[0:128, 2 * q:2 * q + 2], neg_half[0:128, :],
                                ALU.pow).then_inc(rs4_ready, 1)

            def add_b2(q):
                for j in (2 * q, 2 * q + 1):
                    n = PTILES[j][1]
                    pool.wait_ge(h3_ready, j + 2)
                    g.tensor_tensor(h3b[0:n, j, :], h3[0:n, j, :], m0b2_bc[0:n, :], ADD).then_inc(h3b_ready, 1)

            taps(GP_PARTS[1])
            roots4(0)
            add_b2(0)
            taps(len(todo))
            roots4(1)
            add_b2(1)

        @block.scalar
        def _(act):
            a_ = nc.scalar

            def copy(dst, src, **kw):
                return a_.activation(dst, src, ACT.Identity, **kw)

            def line_up(i):
                c, hh = chunks[i]
                act.wait_ge(l_x[c], 16)
                copy(xr[:, i].rearrange("p n (y w) -> p n y w", y=HB),
                     x_pix[:, c, hh * HB:(hh + 1) * HB].rearrange("p y n w -> p n y w")).then_inc(xr_ready, 1)

            def put_xT(i):
                b0 = 2 * (i % 2)
                act.wait_ge(t_x, i + 1)
                copy(xT[:, i].rearrange("p (g n) q -> p g (n q)", g=2), ps[:, b0:b0 + 2, 0:3 * BH]
                     ).then_inc(xT_ready, 1)

            act.wait_ge(const_ready, 1)
            a_.activation(table_row[:, :], ones[:, 0:1], ACT.Sigmoid)
            line_up(0)
            line_up(1)
            put_xT(0)
            line_up(2)
            put_xT(1)
            line_up(3)
            put_xT(2)
            line_up(4)
            put_xT(3)
            act.wait_ge(t_rows, 1)
            copy(fold_rows[:, :], ps[0:2, 7, 0:D]).then_inc(rows_ready, 1)
            act.wait_ge(l_ssm, 48)
            a_.activation(ssm[:, :, :, :], ssm[:, :, :, :], ACT.Sigmoid).then_inc(sig_ready, 1)
            put_xT(4)
            put_xT(5)
            act.wait_ge(t_ms1, 1)
            copy(ms1T[:, 0:3, :], ps[0:2, 7, D:D + 3 * BH].rearrange("p (n q) -> p n q", n=3)).then_inc(ms1T_ready, 1)
            copy(ms1T[:, 3:6, :], ps[0:2, 0, 0:3 * BH].rearrange("p (n q) -> p n q", n=3)).then_inc(ms1T_ready, 1)
            act.wait_ge(const_ready, 6)

            def roots2(q):
                s = slice(2 * q, 2 * q + 2)
                act.wait_ge(var2, q + 1)
                a_.activation(rs2[:, s], ve2[:, s], ACT.Sqrt).then_inc(rs2_ready, 1)

            def roots3(n, s, count):
                act.wait_ge(var3, count)
                a_.activation(s3[0:n, 0, s], ag3[0:n, s, 1], ACT.Sqrt, bias=eps5[0:n, :]).then_inc(rs3_ready, 1)
                a_.activation(s3[0:n, 1, s], ag3[0:n, s, 1], ACT.Sqrt).then_inc(rs3_ready, 1)

            def put_r(n, nws, count):
                act.wait_ge(co_ready, 2 * count)
                for nw in nws:
                    copy(r[0:n, nw, :], h2[0:n, nw, :], bias=nm3[0:n, nw:nw + 1], scale=one3[0:n, nw:nw + 1]
                         ).then_inc(r_ready, 1)

            def put_xnT(q):
                act.wait_ge(t_xs, q + 2)
                c0 = NB + 2 * q * BH
                copy(xnT[0:DH, :, c0:c0 + 2 * BH].rearrange("p h (n q) -> p n h q", n=2),
                     ps[0:DH, q % 2, 0:4 * BH].rearrange("p (n h q) -> p n h q", n=2, h=2)).then_inc(xnT_ready, 1)

            def put_xp(q):
                c0, c1 = xn_cols(q)
                n0 = c1 - c0 - 2 * BH
                for e in range(ET):
                    i = q * ET + e
                    act.wait_ge(t_xp, i + 1)
                    if q == 0:
                        copy(xp[:, e, 0:NB], ps[:, XP_BANK[i], 0:NB]).then_inc(xp_ready, 1)
                    for j in range(2):
                        copy(xp[:, e, NB:NT].rearrange("p (h n b) -> p n h b", h=NH, b=NB)[:, 2 * q + j],
                             ps[:, XP_BANK[i], n0 + j * BH:n0 + (j + 1) * BH].rearrange("p (b h) -> p h b", h=NH)
                             ).then_inc(xp_ready, 1)

            def put_xs(q):
                act.wait_ge(nb_ready, q + 1)
                for nw in pair(q):
                    copy(xs[:, nw, :], h2[:, nw, :], bias=nb3[:, nw:nw + 1], scale=s3[:, 1, nw:nw + 1]
                         ).then_inc(xa_ready, 1)

            roots3(NB, slice(NW, NW + 1), 1)
            roots2(0)
            act.wait_ge(l_gamma, 32)
            for hh in range(2):
                act.wait_ge(t_w, hh + 1)
                copy(WinT[0:DH, hh, :], ps[0:DH, hh, 0:E], scale=gamma_col[:, hh:hh + 1]).then_inc(wT_ready, 1)
            roots3(BH, slice(0, 2), 2)
            roots2(1)
            put_xs(0)
            act.wait_ge(t_xs, 1)
            copy(xnT[0:DH, :, 0:NB], ps[0:DH, 7, 0:2 * NB].rearrange("p (h b) -> p h b", h=2)
                 ).then_inc(xnT_ready, 1)
            roots3(BH, slice(2, 4), 3)
            put_xnT(0)
            roots2(2)
            act.wait_ge(t_w, 3)
            copy(WoutT[:, 0:2, :], ps[:, 4, 0:2 * D].rearrange("p (e d) -> p e d", e=2)).then_inc(wT_ready, 1)
            act.wait_ge(t_w, 4)
            copy(WoutT[:, 2, :], ps[:, 5, 0:D]).then_inc(wT_ready, 1)
            put_xs(1)
            put_xnT(1)
            roots3(BH, slice(4, 6), 4)
            put_xp(0)
            put_r(NB, [NW], 1)
            put_r(BH, pair(0), 2)
            put_xnT(2)
            put_xp(1)
            put_xp(2)

            todo = [(q, k) for q in range(2) for k in GP_TAPS[q]]
            n_prod = [0]

            def taps(n):
                for _ in range(min(n, len(todo))):
                    q, k = todo.pop(0)
                    c0, n_ = HALF[q]
                    lo = max(CT + c0, k * NB) - CT
                    first = k == GP_TAPS[q][0]
                    if not first:
                        if n_prod[0] >= NTMP:
                            act.wait_ge(prod_used, n_prod[0] - NTMP + 1)
                        b = n_prod[0] % NTMP
                        n_prod[0] += 1
                    for e in range(ET):
                        dst = yg[:, e, lo:c0 + n_] if first else ptmp[:, b, e, lo - c0:n_]
                        copy(dst, xp[:, e, CT + lo - k * NB:CT + c0 + n_ - k * NB], scale=Kk[:, k, e:e + 1]
                             ).then_inc(prod_ready, 1)

            act.wait_ge(K_ready, 1)
            act.wait_ge(xp_ready, XP_DONE[ET - 1])
            taps(AC_PARTS[0])
            act.wait_ge(t_x4c, 1)
            copy(x4T[0:DH, :, 0:CT], ps[0:DH, 6, 0:2 * CT].rearrange("p (h t) -> p h t", h=2)).then_inc(x4T_ready, 1)
            for hh in range(2):
                copy(x_par[0:DH, hh, :, 0:CT // 2].rearrange("p j (i b) -> p j i b", b=NB),
                     ps[0:DH, 6, hh * CT:(hh + 1) * CT].rearrange("p (i j b) -> p j i b", j=2, b=NB)
                     ).then_inc(x4T_ready, 1)
            taps(AC_PARTS[1])
            act.wait_ge(gmax_ready, 1)
            a_.activation(g_e[:, :], g_d[:, :], ACT.Exp).then_inc(gexp_ready, 1)
            act.wait_ge(t_uplo, 1)
            a_.activation(hid_lo.rearrange("p (k f) -> p k f", k=2), ps[0:CT, 0:2, 0:HH], ACT.Gelu
                          ).then_inc(hlo_ready, 1)
            taps(AC_PARTS[2])
            act.wait_ge(t_uphi, 1)
            a_.activation(hid_hi.rearrange("p (k f) -> p k f", k=2), ps[:, 6:8, 0:HH], ACT.Gelu
                          ).then_inc(hhi_ready, 1)
            for q in range(2):
                act.wait_ge(t_tlo, q + 1)
                for j in range(2):
                    copy(hid_par[:, M2 * q:M2 * (q + 1), j, 0:CT // 2].rearrange("p m (i b) -> p m i b", b=NB),
                         ps[:, q, 0:M2 * CT].rearrange("p (m i j b) -> p m i j b", m=M2, j=2, b=NB)[:, :, :, j]
                         ).then_inc(hpar_ready, 1)
            for q in range(2):
                act.wait_ge(t_thi, q + 1)
                for j in range(2):
                    copy(hid_cls[:, M2 * q:M2 * (q + 1)].rearrange("p m (i j b) -> p m i j b", j=2, b=NB)[:, :, :, j],
                         ps[:, 6 + q, 0:M2 * 128].rearrange("p (m j t) -> p m j t", m=M2, j=2)[:, :, j, 0:CT // 2]
                         .rearrange("p m (i b) -> p m i b", b=NB)).then_inc(hcls_ready, 1)
            taps(AC_PARTS[3])
            for j, (c0, n) in enumerate(PTILES):
                q = j // 2
                if j % 2 == 0:
                    act.wait_ge(t_x4, q + 1)
                copy(x4T[0:DH, :, CT + c0:CT + c0 + n],
                     ps[0:DH, X4_BANK[q], (j % 2) * 256:(j % 2) * 256 + 2 * n].rearrange("p (h t) -> p h t", h=2)
                     ).then_inc(x4T_ready, 1)
                if j == 1:
                    act.wait_ge(t_dnpar, 1)
                    copy(o_par[:, :], ps[:, 5, 0:D]).then_inc(opar_ready, 1)
                    taps(AC_PARTS[5])
                if j % 2 == 0:
                    continue
                c0, n = HALF[q]
                for m in range(M):
                    i = q * M + m
                    act.wait_ge(t_up, i + 1)
                    a_.activation(hid[:, m, c0:c0 + n], ps[:, UP_BANK[i % 3], 0:n], ACT.Gelu).then_inc(hid_ready, 1)
                    if q == 0:
                        taps(AC_PARTS[4])
                if q == 0:
                    taps(len(todo))

        @block.vector
        def _(dve):
            v = nc.vector
            n_step = [0]

            def step(ins):
                n_step[0] += 1
                ins.then_inc(vec_step, 1)
                return n_step[0]

            v.memset(xnT[DH:DH + 1, 0, :], 1.0).then_inc(pads_ready, 1)
            v.memset(x4T[DH:DH + 1, 0, :], 1.0).then_inc(pads_ready, 1)
            v.memset(x_par[DH:DH + 1, 0, :, :], 1.0).then_inc(pads_ready, 1)
            v.memset(x_par[0:DH, :, :, CT // 2:], 0.0).then_inc(pads_ready, 1)
            v.memset(hid_par[:, :, :, CT // 2:], 0.0).then_inc(pads_ready, 1)
            v.memset(ve4[96:128, 3:4], 1.0).then_inc(pads_ready, 1)

            def norm3_stats(rows, nws):
                for nw in nws:
                    k = step(v.bn_stats(st3[0:rows, nw, :], h2[0:rows, nw, :]))
                dve.wait_ge(vec_step, k)
                for nw in nws:
                    ins = v.bn_aggr(ag3[0:rows, nw, :], st3[0:rows, nw, :])
                ins.then_inc(var3, 1)

            def norm3_apply(rows, nws, count):
                s = slice(nws[0], nws[-1] + 1)
                dve.wait_ge(var3, count)
                dve.wait_ge(rs3_ready, 2 * count)
                k = step(v.scalar_tensor_tensor(s3[0:rows, 1, s], s3[0:rows, 0, s], EPS6, s3[0:rows, 1, s], MUL, ADD))
                dve.wait_ge(vec_step, k)
                v.reciprocal(s3[0:rows, :, s], s3[0:rows, :, s]).then_inc(rc_ready, 1)
                dve.wait_ge(rc_ready, count)
                if count in (2, 3):
                    v.scalar_tensor_tensor(nb3[:, s], ag3[:, s, 0], -1.0, s3[:, 1, s], MUL, MUL).then_inc(nb_ready, 1)
                    return
                for nw in nws:
                    v.tensor_scalar(xs[0:rows, nw, :], h2[0:rows, nw, :], ag3[0:rows, nw, 0:1],
                                    s3[0:rows, 1, nw:nw + 1], SUB, MUL).then_inc(xs_ready, 1)

            for c in range(NC):
                dve.wait_ge(l_x[c], 16)
                for nw in range(NW):
                    k = step(v.bn_stats(st1[:, nw, c, :], x_pix[:, c, :, nw, :]))
                if c == 0:
                    dve.wait_ge(l_ln1, 32)
                    dve.wait_ge(l_W, 16)
                    for cc, hh in chunks:
                        v.tensor_scalar(Wp[:, hh, cc, :], W_sb[:, hh, cc, :], ln1_col[:, 0, hh, cc:cc + 1], None, MUL
                                        ).then_inc(Wp_ready, 1)
            dve.wait_ge(vec_step, k)
            for nw in range(NW):
                ins = v.bn_aggr(ag1[:, nw, :], st1[:, nw].rearrange("p c s -> p (c s)"))
            ins.then_inc(var1, 1)
            dve.wait_ge(var1, 1)
            v.tensor_scalar(ms1[:, :, 0], ag1[:, :, 0], -1.0, None, MUL).then_inc(nm1_ready, 1)
            v.tensor_scalar(ms1[:, :, 1], ag1[:, :, 1], EPS5, None, ADD).then_inc(nm1_ready, 1)
            k = step(v.tensor_scalar(ve1[:, :], ag1[:, :, 1], EPS5, EPS5, ADD, MUL))
            dve.wait_ge(l_cls, 32)
            k = step(v.tensor_tensor(h2[0:NB, NW, :], cls_sb[:, :], pos0_sb[:, :], ADD))
            dve.wait_ge(vec_step, k)
            norm3_stats(NB, [NW])

            def token_rows(q):
                dve.wait_ge(t_h, 2 * q + 2)
                for nw in pair(q):
                    k = step(v.bn_stats(st2[:, nw, :], hbank(nw)))
                dve.wait_ge(vec_step, k)
                for nw in pair(q):
                    k = step(v.bn_aggr(ag2[:, nw, :], st2[:, nw, :]))
                s = slice(2 * q, 2 * q + 2)
                dve.wait_ge(vec_step, k)
                v.tensor_tensor(ve2[:, s], ag2[:, s, 1], ve1[:, s], ADD).then_inc(var2, 1)
                if q == 0:
                    dve.wait_ge(l_ln2, 32)
                for nw in pair(q):
                    v.scalar_tensor_tensor(h[:, nw, :], hbank(nw), ag2[:, nw, 0:1], ln2w_bc[:, :],
                                           SUB, MUL).then_inc(h_read, 1)

            def tokens(q):
                s = slice(2 * q, 2 * q + 2)
                dve.wait_ge(rs2_ready, q + 1)
                k = step(v.reciprocal(rs2[:, s], rs2[:, s]))
                if q == 0:
                    dve.wait_ge(posb_ready, 1)
                dve.wait_ge(vec_step, k)
                dve.wait_ge(h_read, 2 * q + 2)
                for nw in pair(q):
                    k = step(v.scalar_tensor_tensor(h2[:, nw, :], h[:, nw, :], rs2[:, nw:nw + 1], posb[:, nw, :],
                                                    MUL, ADD))
                dve.wait_ge(vec_step, k)
                norm3_stats(BH, pair(q))

            token_rows(0)
            norm3_apply(NB, [NW], 1)
            tokens(0)
            token_rows(1)
            norm3_apply(BH, pair(0), 2)
            tokens(1)
            token_rows(2)
            norm3_apply(BH, pair(1), 3)
            tokens(2)
            norm3_apply(BH, pair(2), 4)
            s = slice(2, 6)
            step(v.tensor_scalar(one3[0:BH, s], s3[0:BH, 0, s], 1.0, None, ADD))
            k = step(v.scalar_tensor_tensor(nm3[0:BH, s], ag3[0:BH, s, 0], -1.0, s3[0:BH, 0, s], MUL, MUL))
            dve.wait_ge(vec_step, k)
            for nw in range(2, NW):
                v.tensor_scalar(r[:, nw, :], h2[:, nw, :], one3[0:BH, nw:nw + 1], nm3[0:BH, nw:nw + 1], MUL, ADD
                                ).then_inc(rv_ready, 1)

            dve.wait_ge(K_ready, 1)

            last = [0] * ET

            def tap(e, k, c0, c1, first):
                lo = max(c0, k * NB)
                dst, src = y[:, e, lo:c1], xp[:, e, lo - k * NB:c1 - k * NB]
                if first:
                    return v.tensor_scalar(dst, src, Kk[:, k, e:e + 1], None, MUL)
                dve.wait_ge(vec_step, last[e])
                return v.scalar_tensor_tensor(dst, src, Kk[:, k, e:e + 1], dst, MUL, ADD)

            for k in range(NCLS):
                for e in range(ET):
                    if k == 0:
                        dve.wait_ge(xp_ready, XP_DONE[e])
                    ins = tap(e, k, 0, CT, k == 0)
                    if k < NCLS - 1:
                        last[e] = step(ins)
                    else:
                        ins.then_inc(ycls_ready, 1)

            todo = [(CT, NT, k, e) for k in VE_BOTH for e in range(ET)]
            for q, (c0, n) in enumerate(HALF):
                todo += [(CT + c0, CT + c0 + n, k, e) for k in VE_TAPS[q] for e in range(ET)]

            def tap_op():
                if todo:
                    c0, c1, k, e = todo.pop(0)
                    last[e] = step(tap(e, k, c0, c1, k == VE_BOTH[0]))

            def taps(n):
                for _ in range(n * ET):
                    tap_op()

            def merge(q):
                c0, n_ = HALF[q]
                for e in range(ET):
                    dst = y[:, e, CT + c0:CT + c0 + n_]
                    dve.wait_ge(t_y, ET * q + e + 1)
                    dve.wait_ge(vec_step, last[e])
                    last[e] = step(v.tensor_tensor(dst, ps[:, Y_BANK[e], c0:c0 + n_], dst, ADD))
                dve.wait_ge(prod_used, sum(len(taps_) - 1 for taps_ in GP_TAPS[:q + 1]))
                for e in range(ET):
                    dst = y[:, e, CT + c0:CT + c0 + n_]
                    dve.wait_ge(vec_step, last[e])
                    v.tensor_tensor(dst, dst, yg[:, e, c0:c0 + n_], ADD).then_inc(y_ready, 1)

            dve.wait_ge(pads_ready, 6)

            def norm4(tiles):
                for j, n, bank, col in tiles:
                    dve.wait_ge(*((t_woc, 1) if j == 4 else (t_wo, (2, 2, 3, 4)[j])))
                    dve.wait_ge(rtok_ready, 1 if j == 4 else j + 2)
                    v.tensor_tensor(h3[0:n, j, :], ps[0:n, bank, col:col + D], r_tok[0:n, j, :], ADD
                                    ).then_inc(h3_ready, 1)
                for j, n, bank, col in tiles:
                    dve.wait_ge(h3_ready, 1 if j == 4 else j + 2)
                    k = step(v.bn_stats(st4[0:n, j, :], h3[0:n, j, :]))
                dve.wait_ge(vec_step, k)
                for j, n, bank, col in tiles:
                    k = step(v.bn_aggr(ag4[0:n, j, :], st4[0:n, j, :]))
                dve.wait_ge(vec_step, k)
                for j, n, bank, col in tiles:
                    v.tensor_scalar(ve4[0:n, j:j + 1], ag4[0:n, j, 1:2], EPS5, None, ADD).then_inc(var4, 1)

            def apply4(j, n):
                dve.wait_ge(rs4_ready, 1 if j == 4 else j // 2 + 2)
                v.tensor_scalar(x4[0:n, j, :], h3[0:n, j, :], ag4[0:n, j, 0:1], rs4[0:n, j:j + 1], SUB, MUL
                                ).then_inc(x4_ready, 1)

            taps(VE_PARTS[0])
            step(v.tensor_reduce(cmask[:, :], ident[0:CT, 0:CT].rearrange("p (i b) -> p i b", b=NB), AX.X, ADD))
            norm4([(4, CT, 5, 0)])
            taps(VE_PARTS[1])
            apply4(4, CT)
            taps(VE_LEFT0)
            dve.wait_ge(t_g, 1)
            k = step(v.tensor_tensor(gsel[:, :, :], ps[0:CT, 5, 0:2 * NCLS].rearrange("p (i j) -> p i j", j=2),
                                     cmask[:, :].unsqueeze(2).broadcast_to([CT, NCLS, 2]), MUL))
            dve.wait_ge(vec_step, k)
            k = step(v.tensor_reduce(lg[:, :], gsel[:, :, :].rearrange("p i j -> p j i"), AX.X, ADD))
            dve.wait_ge(vec_step, k)
            k = step(v.tensor_reduce(g_mx[:, :], lg[:, :], AX.X, ALU.max))
            dve.wait_ge(vec_step, k)
            v.tensor_scalar(g_d[:, :], lg[:, :], g_mx[:, 0:1], None, SUB).then_inc(gmax_ready, 1)
            merge(0)
            taps(VE_PARTS[2])
            norm4([(j, PTILES[j][1], *WO_SLOT[j]) for j in (0, 1)])
            taps(VE_PARTS[3])
            for j in (0, 1):
                apply4(j, PTILES[j][1])
            taps(VE_PARTS[4])
            dve.wait_ge(gexp_ready, 1)
            k = step(v.tensor_reduce(g_s[:, :], g_e[:, :], AX.X, ADD))
            tap_op()
            dve.wait_ge(vec_step, k)
            k = step(v.reciprocal(g_s[:, :], g_s[:, :]))
            tap_op()
            dve.wait_ge(vec_step, k)
            k = step(v.tensor_scalar(g_p[:, :], g_e[:, :], g_s[:, 0:1], None, MUL))
            tap_op()
            dve.wait_ge(vec_step, k)
            k = step(v.tensor_reduce(g_mx[:, :], g_p[:, :], AX.X, ALU.min))
            tap_op()
            dve.wait_ge(vec_step, k)
            k = step(v.tensor_scalar(g_m[:, :], g_p[:, :], g_mx[:, 0:1], None, ALU.is_gt))
            tap_op()
            dve.wait_ge(vec_step, k)
            k = step(v.tensor_tensor(g_p[:, :], g_p[:, :], g_m[:, :], MUL))
            tap_op()
            dve.wait_ge(vec_step, k)
            k = step(v.tensor_reduce(g_s[:, :], g_p[:, :], AX.X, ADD))
            tap_op()
            dve.wait_ge(vec_step, k)
            k = step(v.tensor_scalar(g_s[:, :], g_s[:, :], EPS6, None, ALU.max))
            tap_op()
            dve.wait_ge(vec_step, k)
            k = step(v.reciprocal(g_s[:, :], g_s[:, :]))
            tap_op()
            dve.wait_ge(vec_step, k)
            k = step(v.tensor_scalar(gate[:, :], g_p[:, :], g_s[:, 0:1], None, MUL))
            tap_op()
            dve.wait_ge(vec_step, k)
            taps(VE_PARTS[6])
            dve.wait_ge(t_dncls, 1)
            k = step(v.scalar_tensor_tensor(oc1, ps[0:CT, 0, 0:D], gate[:, 1:2], h3[0:CT, 4, :], MUL, ADD))
            dve.wait_ge(vec_step, k)
            dve.wait_ge(t_oc, 1)
            v.scalar_tensor_tensor(oc, ps[0:CT, 5, 0:D], gate[:, 0:1], oc1, MUL, ADD
                                   ).then_inc(oc_ready, 1)
            taps(VE_PARTS[5])

            def finish(q):
                for j in (2 * q, 2 * q + 1):
                    n = PTILES[j][1]
                    dve.wait_ge(t_dn, j + 1)
                    dve.wait_ge(h3b_ready, j + 1)
                    v.tensor_tensor(o[0:n, j, :], ps[0:n, DN_BANK[j], 0:D], h3b[0:n, j, :], ADD).then_inc(o_ready, 1)

            taps(T)
            merge(1)
            norm4([(j, PTILES[j][1], *WO_SLOT[j]) for j in (2, 3)])
            for j in (2, 3):
                apply4(j, PTILES[j][1])
            finish(0)
            finish(1)

        @block.tensor
        def _(pe):
            t = nc.tensor

            def mm(out_, lhsT, rhs, start, stop):
                return t.matmul(out_, lhsT, rhs, start=start, stop=stop, skip_group_check=True)

            def keep_warm(n, bank):
                for _ in range(n):
                    mm(ps[:, bank, 384:512], ident[:, :], ident[:, :], True, True)

            pe.wait_ge(ident_ready, 1)
            keep_warm(WARM, 7)

            def turn(i):
                pe.wait_ge(*((xr5_ready, 1) if i == KC - 1 else (xr_ready, i + 1)))
                if i >= 2:
                    pe.wait_ge(xT_ready, i - 1)
                for nw in range(NW):
                    ins = t.transpose(ps[:, 2 * (i % 2) + nw // 3, (nw % 3) * BH:(nw % 3 + 1) * BH],
                                      xr[:, i, nw, :], ident[0:BH, 0:BH])
                ins.then_inc(t_x, 1)

            def product(i, nws):
                c, hh = chunks[i]
                pe.wait_ge(Wp_ready, i + 1)
                pe.wait_ge(xT_ready, i + 1)
                for nw in nws:
                    mm(hbank(nw), xT[:, i, nw, :], Wp[:, hh, c, :], i == 0 and nw % 2 == 0, False)

            def fold(nws):
                for nw in nws:
                    mm(hbank(nw), ms1T[:, nw, :], fold_rows[:, :], False, True).then_inc(t_h, 1)

            turn(0)
            turn(1)
            pe.wait_ge(l_ln1, 32)
            pe.wait_ge(l_W, 16)
            for i, (c, hh) in enumerate(chunks):
                mm(ps[0:2, 7, 0:D], ln1_col[:, :, hh, c], W_sb[:, hh, c, :], i == 0, False)
            product(0, [0, 1])
            turn(2)
            product(0, [2, 3])
            product(1, [0, 1])
            pe.wait_ge(const_ready, 6)
            pe.wait_ge(l_tokb, 16)
            mm(ps[0:2, 7, 0:D], sel01[:, :], tokb_row[:, :], False, True).then_inc(t_rows, 1)
            turn(3)
            product(2, [0, 1])
            turn(4)
            product(3, [0, 1])
            turn(5)
            product(4, [0, 1])
            pe.wait_ge(rows_ready, 1)
            pe.wait_ge(nm1_ready, 2)
            pe.wait_ge(rs1_ready, 1)
            for nw in range(NW):
                out_ = ps[0:2, 7, D + nw * BH:D + (nw + 1) * BH] if nw < 3 else ps[0:2, 0, (nw - 3) * BH:(nw - 2) * BH]
                ins = t.transpose(out_, ms1[:, nw, :], ident[0:BH, 0:BH])
            ins.then_inc(t_ms1, 1)
            product(5, [0, 1])
            pe.wait_ge(ms1T_ready, 2)
            fold([0, 1])
            for i in range(1, KC):
                product(i, [2, 3])
            fold([2, 3])
            pe.wait_ge(l_Win, 32)
            for hh in range(2):
                for e in range(ET):
                    ins = t.transpose(ps[0:DH, hh, e * 128:(e + 1) * 128], Win_sb[:, e, hh * DH:(hh + 1) * DH],
                                      ident[:, :])
                ins.then_inc(t_w, 1)
            pe.wait_ge(xs_ready, 1)
            for hh in range(2):
                ins = t.transpose(ps[0:DH, 7, hh * NB:(hh + 1) * NB], xs[0:NB, NW, hh * DH:(hh + 1) * DH],
                                  ident[0:NB, 0:NB])
            ins.then_inc(t_xs, 1)
            for i in range(KC):
                product(i, [4, 5])
            fold([4, 5])

            pe.wait_ge(pads_ready, 6)
            for q in range(NPAIR):
                pe.wait_ge(*((xs_ready, 3) if q == 2 else (xa_ready, 2 * q + 2)))
                for nw in pair(q):
                    for hh in range(2):
                        c0 = (2 * (nw % 2) + hh) * BH
                        ins = t.transpose(ps[0:DH, q % 2, c0:c0 + BH], xs[:, nw, hh * DH:(hh + 1) * DH],
                                          ident[0:BH, 0:BH])
                ins.then_inc(t_xs, 1)
                if q == 0:
                    pe.wait_ge(l_Wout, 16)
                    for e in range(ET):
                        for hh in range(2):
                            c0 = (e % 2) * D + hh * DH
                            ins = t.transpose(ps[:, 4 + e // 2, c0:c0 + DH], Wout_sb[:, hh, e * 128:(e + 1) * 128],
                                              ident[0:DH, 0:DH])
                        if e >= 1:
                            ins.then_inc(t_w, 1)
                pe.wait_ge(xnT_ready, q + 2)
                c0, c1 = xn_cols(q)
                for e in range(ET):
                    i = q * ET + e
                    if i == 0:
                        pe.wait_ge(wT_ready, 2)
                    if i == 3:
                        pe.wait_ge(wT_ready, 4)
                    if i >= 5:
                        pe.wait_ge(xp_ready, {5: 3, 7: 6, 8: 9}.get(i, 3))
                    for hh in range(2):
                        ins = mm(ps[:, XP_BANK[i], 0:c1 - c0], WinT[0:KH[hh], hh, e * 128:(e + 1) * 128],
                                 xnT[0:KH[hh], hh, c0:c1], hh == 0, hh == 1)
                    ins.then_inc(t_xp, 1)

            todo = [(q, k) for q in range(2) for k in PE_TAPS[q]]

            def taps(n):
                for _ in range(min(n, len(todo))):
                    q, k = todo.pop(0)
                    c0, n_ = HALF[q]
                    lo = max(CT + c0, k * NB)
                    first, final = k == PE_TAPS[q][0], k == PE_TAPS[q][-1]
                    for e in range(ET):
                        if first:
                            pe.wait_ge(*((xp_ready, XP_DONE[e]) if q == 0 else (y_ready, e + 1)))
                        pe.wait_ge(diag_ready, DIAGS.index(k) * ET + e + 1)
                        ins = mm(ps[:, Y_BANK[e], lo - CT:c0 + n_], diag[:, DIAGS.index(k), e, :],
                                 xp[:, e, lo - k * NB:CT + c0 + n_ - k * NB], first, final)
                        if final:
                            ins.then_inc(t_y, 1)

            def project(cols, n, bank, col, done):
                for e in range(ET):
                    ins = mm(ps[0:n, bank, col:col + D], y[:, e, cols:cols + n], WoutT[:, e, :], e == 0, e == ET - 1)
                ins.then_inc(done, 1)

            taps(PE_PARTS[0])
            pe.wait_ge(ycls_ready, ET)
            pe.wait_ge(wT_ready, 4)
            project(0, CT, 5, 0, t_woc)
            taps(PE_PARTS[1])
            pe.wait_ge(x4_ready, 1)
            for hh in range(2):
                ins = t.transpose(ps[0:DH, 6, hh * CT:(hh + 1) * CT], x4[0:CT, 4, hh * DH:(hh + 1) * DH],
                                  ident[0:CT, 0:CT])
            ins.then_inc(t_x4c, 1)
            taps(PE_PARTS[2])
            pe.wait_ge(x4T_ready, 3)
            pe.wait_ge(l_G, 32)
            for hh in range(2):
                ins = mm(ps[0:CT, 5, 0:2 * NCLS], x4T[0:DH, hh, 0:CT], G_sb[:, hh].rearrange("p i j -> p (i j)"),
                         hh == 0, hh == 1)
            ins.then_inc(t_g, 1)

            def turn_x4(q):
                for j in (2 * q, 2 * q + 1):
                    n = PTILES[j][1]
                    pe.wait_ge(x4_ready, j + 2)
                    for hh in range(2):
                        c0 = (j % 2) * 256 + hh * n
                        ins = t.transpose(ps[0:DH, X4_BANK[q], c0:c0 + n], x4[0:n, j, hh * DH:(hh + 1) * DH],
                                          ident[0:n, 0:n])
                ins.then_inc(t_x4, 1)

            def up(q):
                h0, hn = HALF[q]
                pe.wait_ge(x4T_ready, 3 + 2 * (q + 1))
                for m in range(M):
                    i = q * M + m
                    if i >= len(UP_BANK):
                        pe.wait_ge(hid_ready, i - len(UP_BANK) + 1)
                    for hh in range(2):
                        ins = mm(ps[:, UP_BANK[i % 3], 0:hn], W1_sb[0:KH[hh], hh, m * 128:(m + 1) * 128],
                                 x4T[0:KH[hh], hh, CT + h0:CT + h0 + hn], hh == 0, hh == 1)
                    ins.then_inc(t_up, 1)

            def down(j, ms):
                c0, n = PTILES[j]
                for m in ms:
                    pe.wait_ge(hid_ready, (j // 2) * M + m + 1)
                    ins = mm(ps[0:n, DN_BANK[j], 0:D], hid[:, m, c0:c0 + n], W2_sb[:, m, :], m == 0, m == M - 1)
                if ms[-1] == M - 1:
                    ins.then_inc(t_dn, 1)

            pe.wait_ge(l_A1, 16 * (NEXP + 1))
            for k in range(2):
                for hh in range(2):
                    for a in range(NLO):
                        ins = mm(ps[32 * a:32 * a + 32, k, 0:HH], x4T[0:KH[hh], hh, 32 * a:32 * a + 32],
                                 A1_sb[0:KH[hh], a, hh, k * HH:(k + 1) * HH], hh == 0, hh == 1)
            ins.then_inc(t_uplo, 1)
            for k in range(2):
                for hh in range(2):
                    for a in range(NHI):
                        ins = mm(ps[64 * a:64 * a + 64, 6 + k, 0:HH], x_par[0:KH[hh], hh, a, :],
                                 A1_sb[0:KH[hh], NLO + a, hh, k * HH:(k + 1) * HH], hh == 0, hh == 1)
            ins.then_inc(t_uphi, 1)
            pe.wait_ge(y_ready, ET)
            pe.wait_ge(gmax_ready, 1)
            for j in (0, 1):
                project(CT + PTILES[j][0], PTILES[j][1], *WO_SLOT[j], t_wo)
            pe.wait_ge(hlo_ready, 1)
            for m in range(M):
                ins = t.transpose(ps[:, m // M2, (m % M2) * CT:(m % M2 + 1) * CT], hid_lo[:, m * 128:(m + 1) * 128],
                                  ident[0:CT, 0:CT])
                if m % M2 == M2 - 1:
                    ins.then_inc(t_tlo, 1)
            taps(PE_PARTS[3])
            pe.wait_ge(hhi_ready, 1)
            for m in range(M):
                ins = t.transpose(ps[:, 6 + m // M2, (m % M2) * 128:(m % M2 + 1) * 128],
                                  hid_hi[:, m * 128:(m + 1) * 128], ident[:, :])
                if m % M2 == M2 - 1:
                    ins.then_inc(t_thi, 1)
            taps(PE_PARTS[4])
            pe.wait_ge(l_A2, 16 * NEXP)
            pe.wait_ge(l_A2b, 16)
            pe.wait_ge(h3_ready, 3)
            pe.wait_ge(hpar_ready, 4)
            for m in range(M):
                for j in range(NHI):
                    mm(ps[64 * j:64 * j + 64, 5, 0:D], hid_par[:, m, j, :], A2_sb[:, NLO + j, m, :], m == 0, False)
            for j in range(NHI):
                ins = mm(ps[64 * j:64 * j + 64, 5, 0:D], ones[:, 0:64], A2b_row[:, NLO + j, :], False, True)
            ins.then_inc(t_dnpar, 1)
            turn_x4(0)
            pe.wait_ge(hcls_ready, 4)
            for m in range(M):
                for c in range(NLO):
                    mm(ps[32 * c:32 * c + 32, 0, 0:D], hid_cls[:, m, 32 * c:32 * c + 32], A2_sb[:, c, m, :],
                       m == 0, False)
            for c in range(NLO):
                ins = mm(ps[32 * c:32 * c + 32, 0, 0:D], ones[:, 0:32], A2b_row[:, c, :], False, True)
            ins.then_inc(t_dncls, 1)

            pe.wait_ge(opar_ready, 1)
            pe.wait_ge(perm_ready, 2)
            mm(ps[0:CT, 5, 0:D], perm[:, :, :, :].rearrange("p i j b -> p (i j b)"), o_par[:, :], True, True
               ).then_inc(t_oc, 1)
            pe.wait_ge(l_W1, 32)
            up(0)
            taps(len(todo))
            pe.wait_ge(hid_ready, M)
            keep_warm(GAP_WARM, 7)
            for e in range(ET):
                pe.wait_ge(y_ready, ET + e + 1)
                for j in (2, 3):
                    c0, n = PTILES[j]
                    ins = mm(ps[0:n, WO_SLOT[j][0], 0:D], y[:, e, CT + c0:CT + c0 + n], WoutT[:, e, :],
                             e == 0, e == ET - 1)
                    if e == ET - 1:
                        ins.then_inc(t_wo, 1)
            pe.wait_ge(l_W2, 16)
            pe.wait_ge(oc_ready, 1)
            every = list(range(M))
            down(0, every)
            down(1, every[:M2])
            turn_x4(1)
            down(1, every[M2:])
            up(1)
            down(2, every)
            down(3, every)


_INS = ['x', 'L0_tok_ln1_w', 'L0_tok_ln1_b', 'L0_tok_W', 'L0_tok_b', 'L0_tok_ln2_w', 'L0_tok_ln2_b',
        'L0_tok_cls', 'L0_tok_pos', 'L0_attn_gamma', 'L0_attn_W_in', 'L0_attn_b_in', 'L0_attn_conv_w',
        'L0_attn_A', 'L0_attn_Bp', 'L0_attn_C', 'L0_attn_W_out', 'L0_attn_b_out', 'L0_ffn_moe0_W1',
        'L0_ffn_moe0_b1', 'L0_ffn_moe0_W2', 'L0_ffn_moe0_b2', 'L0_ffn_A1_W', 'L0_ffn_A1_b', 'L0_ffn_A2_W',
        'L0_ffn_A2_b', 'L0_ffn_G_W']


def kernel(**inputs):
    import numpy as _np
    import concourse.bacc as _bacc
    from concourse import mybir as _mybir
    from concourse.bass_utils import run_bass_kernel_spmd as _run

    nc = _bacc.Bacc("TRN2", target_bir_lowering=False, num_devices=1)
    arrays, args = {}, []
    for name in _INS:
        a = _np.ascontiguousarray(inputs[name])
        arrays[f"in_{name}_dram"] = a
        args.append(nc.dram_tensor(f"in_{name}_dram", a.shape, _mybir.dt.from_np(a.dtype), kind="ExternalInput").ap())
    shape = (inputs['x'].shape[0], 37, 192)
    args.append(nc.dram_tensor("out_0_dram", shape, _mybir.dt.float32, kind="ExternalOutput").ap())
    vit_tower_kernel(nc, *args)
    res = _run(nc, [arrays], core_ids=[0])
    return res.results[0]["out_0_dram"]
```
